# Optimizing a Trainium2 kernel written in Bass

```python
import numpy as np
import jax
import jax.numpy as jnp

def _softmax(x, axis=-1):
    return jax.nn.softmax(x, axis=axis)

def _gelu(x):
    return jax.nn.gelu(x, approximate=True)

def _silu(x):
    return jax.nn.silu(x)

def _sigmoid(x):
    return jax.nn.sigmoid(x)

def _layernorm(x, axis=-1, eps=1e-05):
    m = jnp.mean(x, axis=axis, keepdims=True)
    v = jnp.var(x, axis=axis, keepdims=True)
    return (x - m) / jnp.sqrt(v + eps)

def _scatter_add(tgt, idx, src, axis=0):
    return tgt.at[idx].add(src)

def _segment_sum(src, seg, n):
    return jax.ops.segment_sum(src, seg, n)
kernel_name = 'mk_decoder_postln_d4_seqx_r8_b44de6'

def setup_inputs(seed: int=0):
    np.random.seed(seed)
    _w = jnp.asarray

    def _rec_inputs():
        import jax
        import jax.numpy as jnp
        _rk = jax.random.key(seed)
        x = -0.0002928 + 1 * jax.random.normal(jax.random.fold_in(_rk, 1), (4, 512, 128), jnp.float32)
        _lenS = 512 - jax.random.randint(jax.random.fold_in(_rk, 7), (4,), 0, max(1, 512 // 4) + 1, jnp.int32)
        _lenS2 = 77 - jax.random.randint(jax.random.fold_in(_rk, 8), (4,), 0, max(1, 77 // 4) + 1, jnp.int32)
        _ctx_1024P = jax.random.normal(jax.random.fold_in(_rk, 11), (4, 16, 128), jnp.float32)
        _ctx_1024c = jax.random.dirichlet(jax.random.fold_in(_rk, 511), 0.3 * jnp.ones((16,), jnp.float32), (4, 77))
        _ctx_1024t = jnp.einsum('bsk,bkd->bsd', _ctx_1024c, _ctx_1024P)
        _ctx_1024t = _ctx_1024t * jax.lax.rsqrt(jnp.mean(jnp.square(_ctx_1024t)) + 1e-12) * 0.953939
        ctx_1024 = -1.39393e-06 + 0.999914 * (_ctx_1024t + 0.3 * jax.random.normal(jax.random.fold_in(_rk, 611), (4, 77, 128), jnp.float32))
        _validS = jnp.arange(512)[None, :] < _lenS[:, None]
        _validS2 = jnp.arange(77)[None, :] < _lenS2[:, None]
        _causal = jnp.tril(jnp.ones((512, 512), dtype=bool))
        mask_1x1xSxS2_ik0 = jnp.where(jnp.broadcast_to(_validS2[0:1, None, None, :], (1, 1, 512, 77)), 0, 1).astype(jnp.int32)
        return (x, ctx_1024, mask_1x1xSxS2_ik0)
    x, ctx_1024, mask_1x1xSxS2_ik0 = _rec_inputs()

    def _L0_attn_setup():
        import jax, jax.numpy as jnp
        import numpy as np
        D_MODEL = 128
        NHEAD = 16
        D_HEAD = D_MODEL // NHEAD
        THETA = 10000.0

        def _apply_rope(Q, K):
            B, H, T, D = Q.shape
            qr, qi = (Q.reshape(B, H, T, D // 2, 2)[..., 0], Q.reshape(B, H, T, D // 2, 2)[..., 1])
            kr, ki = (K.reshape(B, H, T, D // 2, 2)[..., 0], K.reshape(B, H, T, D // 2, 2)[..., 1])
            freqs = jnp.arange(D // 2, dtype=jnp.float32) * (1.0 / THETA)
            angles = jnp.arange(T, dtype=jnp.float32)[:, None] * freqs[None, :]
            cos = jnp.cos(angles)[None, None]
            sin = jnp.sin(angles)[None, None]
            qr2 = qr * cos - qi * sin
            qi2 = qr * sin + qi * cos
            kr2 = kr * cos - ki * sin
            ki2 = kr * sin + ki * cos
            Q2 = jnp.stack([qr2, qi2], axis=-1).reshape(B, H, T, D)
            K2 = jnp.stack([kr2, ki2], axis=-1).reshape(B, H, T, D)
            return (Q2, K2)
        key = jax.random.key(seed)
        ks = jax.random.split(key, 9)
        B, T = (4, 256)
        s = 1.0 / np.sqrt(D_MODEL)
        inp = {'x': jax.random.normal(ks[0], (B, T, D_MODEL), dtype=jnp.float32), 'Wq': jax.random.normal(ks[1], (D_MODEL, D_MODEL), dtype=jnp.float32) * s, 'bq': jnp.zeros((D_MODEL,), dtype=jnp.float32), 'Wk': jax.random.normal(ks[2], (D_MODEL, D_MODEL), dtype=jnp.float32) * s, 'bk': jnp.zeros((D_MODEL,), dtype=jnp.float32), 'Wv': jax.random.normal(ks[3], (D_MODEL, D_MODEL), dtype=jnp.float32) * s, 'bv': jnp.zeros((D_MODEL,), dtype=jnp.float32), 'Wo': jax.random.normal(ks[4], (D_MODEL, D_MODEL), dtype=jnp.float32) * s, 'bo': jnp.zeros((D_MODEL,), dtype=jnp.float32)}
        return inp
    _L0_attn_all = _L0_attn_setup()
    _L0_attn_in = {k: v for k, v in _L0_attn_all.items() if k in ('Wq', 'bq', 'Wk', 'bk', 'Wv', 'bv', 'Wo', 'bo')}
    del _L0_attn_all

    def _L0_xattn_setup():
        import jax, jax.numpy as jnp
        import numpy as np
        B, S, SC, E, H = (2, 256, 256, 128, 16)
        D = E // H
        EPS = 1e-06

        def _layernorm(x, g, b):
            m = jnp.mean(x, axis=-1, keepdims=True)
            v = jnp.mean((x - m) ** 2, axis=-1, keepdims=True)
            return (x - m) / jnp.sqrt(v + EPS) * g + b

        def _mha(xk, xv, xq, Wk, Wv, Wq, Wo, bo, masked):
            K = jnp.einsum('bse,hed->bhsd', xk, Wk)
            V = jnp.einsum('bse,hed->bhsd', xv, Wv)
            Q = jnp.einsum('bqe,hed->bhqd', xq, Wq)
            scores = jnp.einsum('bhqd,bhkd->bhqk', Q, K)
            sk = xk.shape[1]
            if masked:
                causal = jnp.triu(jnp.ones((xq.shape[1], sk), dtype=bool), k=1)
                scores = jnp.where(causal, -jnp.inf, scores)
            att = jax.nn.softmax(scores / jnp.sqrt(jnp.asarray(sk, scores.dtype)), axis=-1)
            out = jnp.einsum('bhqk,bhkd->bhqd', att, V)
            out = out.transpose(0, 2, 1, 3).reshape(out.shape[0], out.shape[2], -1)
            return jax.nn.relu(out @ Wo + bo)
        key = jax.random.key(seed)
        ks = jax.random.split(key, 16)
        w = lambda k, shape: jax.random.normal(k, shape, jnp.float32) * 0.02
        return {'inputs': jax.random.normal(ks[0], (B, S, E), jnp.float32), 'context_seq': jax.random.normal(ks[1], (B, SC, E), jnp.float32), 'Wk1': w(ks[2], (H, E, D)), 'Wv1': w(ks[3], (H, E, D)), 'Wq1': w(ks[4], (H, E, D)), 'Wo1': w(ks[5], (E, E)), 'bo1': jnp.zeros((E,), jnp.float32), 'Wk2': w(ks[6], (H, E, D)), 'Wv2': w(ks[7], (H, E, D)), 'Wq2': w(ks[8], (H, E, D)), 'Wo2': w(ks[9], (E, E)), 'bo2': jnp.zeros((E,), jnp.float32), 'Wf': w(ks[10], (E, E)), 'bf': jnp.zeros((E,), jnp.float32), 'g1': jnp.ones((E,), jnp.float32), 'b1': jnp.zeros((E,), jnp.float32), 'g2': jnp.ones((E,), jnp.float32), 'b2': jnp.zeros((E,), jnp.float32), 'g3': jnp.ones((E,), jnp.float32), 'b3': jnp.zeros((E,), jnp.float32)}
    _L0_xattn_all = _L0_xattn_setup()
    _L0_xattn_in = {k: v for k, v in _L0_xattn_all.items() if k in ('Wk1', 'Wv1', 'Wq1', 'Wo1', 'bo1', 'Wk2', 'Wv2', 'Wq2', 'Wo2', 'bo2', 'Wf', 'bf', 'g1', 'b1', 'g2', 'b2', 'g3', 'b3')}
    del _L0_xattn_all

    def _L0_ffn_setup():
        import jax, jax.numpy as jnp
        import numpy as np
        EPS_RMS = 1e-06
        EPS_ACT = 1e-05

        def simple_rms_norm(x):
            ms = jnp.mean(jnp.square(x), axis=-1, keepdims=True)
            return x * jax.lax.rsqrt(ms + EPS_RMS)

        def activation_quant(x):
            absmax = jnp.max(jnp.abs(jax.lax.stop_gradient(x)), axis=-1, keepdims=True)
            scale = 127.0 / jnp.clip(absmax, EPS_ACT, None)
            q = jnp.clip(jnp.round(x * scale), -128.0, 127.0) / scale
            return x + jax.lax.stop_gradient(q - x)
        key = jax.random.key(seed)
        k1, k2, k3 = jax.random.split(key, 3)
        B, S, D_IN, D_OUT = (8, 1024, 128, 128)
        x = jax.random.normal(k1, (B, S, D_IN), dtype=jnp.float32)
        w_int8 = jax.random.randint(k2, (D_OUT, D_IN), -128, 128, dtype=jnp.int32)
        weight_scale = jnp.float32(127.0 / 0.06)
        bias = jax.random.normal(k3, (D_OUT,), dtype=jnp.float32) * 0.01
        return {'x': x, 'w_int8': w_int8, 'weight_scale': weight_scale, 'bias': bias}
    _L0_ffn_all = _L0_ffn_setup()
    _L0_ffn_in = {k: v for k, v in _L0_ffn_all.items() if k in ('w_int8', 'weight_scale', 'bias')}
    del _L0_ffn_all

    def _L1_attn_setup():
        import jax, jax.numpy as jnp
        import numpy as np
        DIM = 128
        NUM_HEADS = 16
        HEAD_DIM = DIM // NUM_HEADS
        TAU = 1.0
        LAMBDA_JUMP = 0.6
        LAMBDA_LOCAL = 0.4
        MIN_ENTROPY = 0.5
        WINDOW = 3
        EPS = 1e-10

        def local_diffusion_kernel(seq_len, strength, window=WINDOW):
            i = jnp.arange(seq_len)
            d = i[:, None] - i[None, :]
            k = jnp.where(jnp.abs(d) <= window, jnp.exp(-d.astype(jnp.float32) ** 2 / (2.0 * strength ** 2)), 0.0)
            return k / (k.sum(axis=-1, keepdims=True) + EPS)
        key = jax.random.key(seed)
        ks = jax.random.split(key, 9)
        scale = 0.02
        x = jax.random.normal(ks[0], (2, 256, DIM), dtype=jnp.float32)
        Wq = jax.random.normal(ks[1], (DIM, DIM), dtype=jnp.float32) * scale
        bq = jax.random.normal(ks[2], (DIM,), dtype=jnp.float32) * scale
        Wk = jax.random.normal(ks[3], (DIM, DIM), dtype=jnp.float32) * scale
        bk = jax.random.normal(ks[4], (DIM,), dtype=jnp.float32) * scale
        Wv = jax.random.normal(ks[5], (DIM, DIM), dtype=jnp.float32) * scale
        bv = jax.random.normal(ks[6], (DIM,), dtype=jnp.float32) * scale
        Wo = jax.random.normal(ks[7], (DIM, DIM), dtype=jnp.float32) * scale
        bo = jax.random.normal(ks[8], (DIM,), dtype=jnp.float32) * scale
        return {'x': x, 'Wq': Wq, 'bq': bq, 'Wk': Wk, 'bk': bk, 'Wv': Wv, 'bv': bv, 'Wo': Wo, 'bo': bo}
    _L1_attn_all = _L1_attn_setup()
    _L1_attn_in = {k: v for k, v in _L1_attn_all.items() if k in ('Wq', 'bq', 'Wk', 'bk', 'Wv', 'bv', 'Wo', 'bo')}
    del _L1_attn_all

    def _L1_xattn_setup():
        import jax, jax.numpy as jnp
        import numpy as np
        NEG_INF = -10000000000.0
        D_MODEL = 128
        NUM_HEADS = 16
        HEAD_DIM = D_MODEL // NUM_HEADS
        B, S = (2, 256)

        def _split_heads(x):
            b, s, _ = x.shape
            return x.reshape(b, s, NUM_HEADS, HEAD_DIM).transpose(0, 2, 1, 3)
        key = jax.random.key(seed)
        ks = jax.random.split(key, 12)
        std = 1.0 / np.sqrt(D_MODEL)
        inp = {'query': jax.random.normal(ks[0], (B, S, D_MODEL), jnp.float32), 'key': jax.random.normal(ks[1], (B, S, D_MODEL), jnp.float32), 'value': jax.random.normal(ks[2], (B, S, D_MODEL), jnp.float32), 'mask': jnp.tril(jnp.ones((S, S), jnp.int32))[None, None, :, :], 'Wq': jax.random.normal(ks[3], (D_MODEL, D_MODEL), jnp.float32) * std, 'bq': jax.random.normal(ks[4], (D_MODEL,), jnp.float32) * std, 'Wk': jax.random.normal(ks[5], (D_MODEL, D_MODEL), jnp.float32) * std, 'bk': jax.random.normal(ks[6], (D_MODEL,), jnp.float32) * std, 'Wv': jax.random.normal(ks[7], (D_MODEL, D_MODEL), jnp.float32) * std, 'bv': jax.random.normal(ks[8], (D_MODEL,), jnp.float32) * std, 'Wo': jax.random.normal(ks[9], (D_MODEL, D_MODEL), jnp.float32) * std, 'bo': jax.random.normal(ks[10], (D_MODEL,), jnp.float32) * std}
        return inp
    _L1_xattn_all = _L1_xattn_setup()
    _L1_xattn_in = {k: v for k, v in _L1_xattn_all.items() if k in ('Wq', 'bq', 'Wk', 'bk', 'Wv', 'bv', 'Wo', 'bo')}
    del _L1_xattn_all

    def _L1_ffn_setup():
        import jax, jax.numpy as jnp
        import numpy as np
        H, E, DFF = (128, 8, 512)
        key = jax.random.key(seed)
        ks = jax.random.split(key, 7)
        s = lambda *shape: 1.0 / np.sqrt(shape[-2] if len(shape) > 1 else shape[-1])
        x = jax.random.normal(ks[0], (2, 256, H), dtype=jnp.float32)
        Wr = jax.random.normal(ks[1], (H, E), dtype=jnp.float32) * (1.0 / np.sqrt(H))
        br = jnp.zeros((E,), dtype=jnp.float32)
        W1 = jax.random.normal(ks[2], (E, H, DFF), dtype=jnp.float32) * (1.0 / np.sqrt(H))
        b1 = jnp.zeros((E, DFF), dtype=jnp.float32)
        W2 = jax.random.normal(ks[3], (E, DFF, H), dtype=jnp.float32) * (1.0 / np.sqrt(DFF))
        b2 = jnp.zeros((E, H), dtype=jnp.float32)
        return {'x': x, 'Wr': Wr, 'br': br, 'W1': W1, 'b1': b1, 'W2': W2, 'b2': b2}
    _L1_ffn_all = _L1_ffn_setup()
    _L1_ffn_in = {k: v for k, v in _L1_ffn_all.items() if k in ('Wr', 'br', 'W1', 'b1', 'W2', 'b2')}
    del _L1_ffn_all

    def _L2_attn_setup():
        import jax, jax.numpy as jnp
        import numpy as np
        B, S, SE, H, NH = (1, 256, 256, 128, 16)
        HD = H // NH
        INNER = 4 * H
        EPS = 1e-05

        def layer_norm(x, g, b):
            mu = jnp.mean(x, axis=-1, keepdims=True)
            var = jnp.mean(jnp.square(x - mu), axis=-1, keepdims=True)
            return (x - mu) * jax.lax.rsqrt(var + EPS) * g + b

        def split_heads(x):
            b, t, _ = x.shape
            return x.reshape(b, t, NH, HD).transpose(0, 2, 1, 3)

        def merge_heads(x):
            b, nh, t, hd = x.shape
            return x.transpose(0, 2, 1, 3).reshape(b, t, nh * hd)

        def _attn_core(q, k, v, extra_bias=None, causal_bool=False, tril_diag2_additive=False):
            w = jnp.einsum('bhqd,bhkd->bhqk', q, k) / jnp.sqrt(jnp.asarray(HD, q.dtype))
            ql, kl = (q.shape[-2], k.shape[-2])
            neg = jnp.finfo(w.dtype).min
            if causal_bool:
                mask = jnp.tril(jnp.ones((ql, kl), bool))
                w = jnp.where(mask[None, None], w, neg)
            if tril_diag2_additive:
                cm = jnp.tril(jnp.ones((ql, kl), w.dtype), k=2)
                w = w + jnp.where(cm == 0, neg, jnp.zeros((), w.dtype))[None, None]
            if extra_bias is not None:
                w = w + extra_bias[:, None, None, :]
            w = jax.nn.softmax(w, axis=-1)
            return jnp.einsum('bhqk,bhkd->bhqd', w, v)
        key = jax.random.key(seed)
        ks = jax.random.split(key, 16)
        n = lambda k, shp: jax.random.normal(k, shp, jnp.float32) * 0.02
        return {'hidden_states': jax.random.normal(ks[0], (B, S, H), jnp.float32), 'encoder_hidden_states': jax.random.normal(ks[1], (B, SE, H), jnp.float32), 'scorer_logits': jax.random.normal(ks[2], (B, SE), jnp.float32), 'ln1_g': jnp.ones((H,), jnp.float32), 'ln1_b': jnp.zeros((H,), jnp.float32), 'c_attn_w': n(ks[3], (H, 3 * H)), 'c_attn_b': jnp.zeros((3 * H,), jnp.float32), 'attn_proj_w': n(ks[4], (H, H)), 'attn_proj_b': jnp.zeros((H,), jnp.float32), 'lnx_g': jnp.ones((H,), jnp.float32), 'lnx_b': jnp.zeros((H,), jnp.float32), 'q_attn_w': n(ks[5], (H, H)), 'q_attn_b': jnp.zeros((H,), jnp.float32), 'x_kv_w': n(ks[6], (H, 2 * H)), 'x_kv_b': jnp.zeros((2 * H,), jnp.float32), 'x_proj_w': n(ks[7], (H, H)), 'x_proj_b': jnp.zeros((H,), jnp.float32), 'ln2_g': jnp.ones((H,), jnp.float32), 'ln2_b': jnp.zeros((H,), jnp.float32), 'fc_w': n(ks[8], (H, INNER)), 'fc_b': jnp.zeros((INNER,), jnp.float32), 'mlp_proj_w': n(ks[9], (INNER, H)), 'mlp_proj_b': jnp.zeros((H,), jnp.float32)}
    _L2_attn_all = _L2_attn_setup()
    _L2_attn_in = {k: v for k, v in _L2_attn_all.items() if k in ('encoder_hidden_states', 'scorer_logits', 'ln1_g', 'ln1_b', 'c_attn_w', 'c_attn_b', 'attn_proj_w', 'attn_proj_b', 'lnx_g', 'lnx_b', 'q_attn_w', 'q_attn_b', 'x_kv_w', 'x_kv_b', 'x_proj_w', 'x_proj_b', 'ln2_g', 'ln2_b', 'fc_w', 'fc_b', 'mlp_proj_w', 'mlp_proj_b')}
    del _L2_attn_all

    def _L2_xattn_setup():
        import jax, jax.numpy as jnp
        import numpy as np
        HIDDEN = 128
        NUM_HEADS = 16
        HEAD_DIM = HIDDEN // NUM_HEADS
        SCALE = 1.0 / float(np.sqrt(HEAD_DIM))
        key = jax.random.key(seed)
        ks = jax.random.split(key, 10)
        B, SQ, SKV = (2, 256, 512)
        init = 0.02
        return {'query_states': jax.random.normal(ks[0], (B, SQ, HIDDEN), dtype=jnp.float32), 'key_value_states': jax.random.normal(ks[1], (B, SKV, HIDDEN), dtype=jnp.float32), 'Wq': jax.random.normal(ks[2], (HIDDEN, HIDDEN), dtype=jnp.float32) * init, 'bq': jnp.zeros((HIDDEN,), dtype=jnp.float32), 'Wk': jax.random.normal(ks[3], (HIDDEN, HIDDEN), dtype=jnp.float32) * init, 'bk': jnp.zeros((HIDDEN,), dtype=jnp.float32), 'Wv': jax.random.normal(ks[4], (HIDDEN, HIDDEN), dtype=jnp.float32) * init, 'bv': jnp.zeros((HIDDEN,), dtype=jnp.float32), 'Wo': jax.random.normal(ks[5], (HIDDEN, HIDDEN), dtype=jnp.float32) * init, 'bo': jnp.zeros((HIDDEN,), dtype=jnp.float32)}
    _L2_xattn_all = _L2_xattn_setup()
    _L2_xattn_in = {k: v for k, v in _L2_xattn_all.items() if k in ('Wq', 'bq', 'Wk', 'bk', 'Wv', 'bv', 'Wo', 'bo')}
    del _L2_xattn_all

    def _L2_ffn_setup():
        import jax, jax.numpy as jnp
        import numpy as np
        D_MODEL = 128
        D_HIDDEN = 512
        NUM_BANKS = 16
        NUM_SELECTED = 2
        key = jax.random.key(seed)
        ks = jax.random.split(key, 7)
        s = 0.02
        return {'tensor': jax.random.normal(ks[0], (4, 128, D_MODEL), dtype=jnp.float32), 'Wr': jax.random.normal(ks[1], (D_MODEL, NUM_BANKS), dtype=jnp.float32) * s, 'br': jnp.zeros((NUM_BANKS,), dtype=jnp.float32), 'W1': jax.random.normal(ks[2], (NUM_BANKS, D_MODEL, D_HIDDEN), dtype=jnp.float32) * s, 'b1': jnp.zeros((NUM_BANKS, D_HIDDEN), dtype=jnp.float32), 'W2': jax.random.normal(ks[3], (NUM_BANKS, D_HIDDEN, D_MODEL), dtype=jnp.float32) * s, 'b2': jnp.zeros((NUM_BANKS, D_MODEL), dtype=jnp.float32)}
    _L2_ffn_all = _L2_ffn_setup()
    _L2_ffn_in = {k: v for k, v in _L2_ffn_all.items() if k in ('Wr', 'br', 'W1', 'b1', 'W2', 'b2')}
    del _L2_ffn_all

    def _L3_attn_setup():
        import jax, jax.numpy as jnp
        import numpy as np
        S, B, F = (256, 2, 128)
        H, D = (16, 64)
        P = H * D
        key = jax.random.key(seed)
        k1, k2, k3 = jax.random.split(key, 3)
        return {'src': jax.random.normal(k1, (S, B, F), dtype=jnp.float32), 'in_proj_weight': jax.random.normal(k2, (3 * P, F), dtype=jnp.float32) * (1.0 / np.sqrt(F)), 'in_proj_bias': jnp.zeros((3 * P,), dtype=jnp.float32), 'out_proj_weight': jax.random.normal(k3, (F, P), dtype=jnp.float32) * (1.0 / np.sqrt(P)), 'out_proj_bias': jnp.zeros((F,), dtype=jnp.float32)}
    _L3_attn_all = _L3_attn_setup()
    _L3_attn_in = {k: v for k, v in _L3_attn_all.items() if k in ('in_proj_weight', 'in_proj_bias', 'out_proj_weight', 'out_proj_bias')}
    del _L3_attn_all

    def _L3_xattn_setup():
        import jax, jax.numpy as jnp
        import numpy as np
        D_MODEL = 128
        NUM_HEADS = 16
        HEAD_DIM = D_MODEL // NUM_HEADS
        SCALE = HEAD_DIM ** (-0.5)
        B, S = (2, 256)
        key = jax.random.key(seed)
        ks = jax.random.split(key, 11)
        s = 1.0 / np.sqrt(D_MODEL)
        inp = {'query': jax.random.normal(ks[0], (B, S, D_MODEL), jnp.float32), 'key': jax.random.normal(ks[1], (B, S, D_MODEL), jnp.float32), 'value': jax.random.normal(ks[2], (B, S, D_MODEL), jnp.float32), 'Wq': jax.random.normal(ks[3], (D_MODEL, D_MODEL), jnp.float32) * s, 'bq': jnp.zeros((D_MODEL,), jnp.float32), 'Wk': jax.random.normal(ks[4], (D_MODEL, D_MODEL), jnp.float32) * s, 'bk': jnp.zeros((D_MODEL,), jnp.float32), 'Wv': jax.random.normal(ks[5], (D_MODEL, D_MODEL), jnp.float32) * s, 'bv': jnp.zeros((D_MODEL,), jnp.float32), 'Wo': jax.random.normal(ks[6], (D_MODEL, D_MODEL), jnp.float32) * s, 'bo': jnp.zeros((D_MODEL,), jnp.float32)}
        return inp
    _L3_xattn_all = _L3_xattn_setup()
    _L3_xattn_in = {k: v for k, v in _L3_xattn_all.items() if k in ('Wq', 'bq', 'Wk', 'bk', 'Wv', 'bv', 'Wo', 'bo')}
    del _L3_xattn_all

    def _L3_ffn_setup():
        import jax, jax.numpy as jnp
        import numpy as np
        B, S, DIM = (4, 256, 128)
        INTER = int(int(DIM * 4) * 0.25)
        E = 32 - 1
        K = 4 - 1

        def _gelu(t):
            return jax.nn.gelu(t, approximate=False)
        key = jax.random.key(seed)
        ks = jax.random.split(key, 12)
        s = 0.02
        return {'x': jax.random.normal(ks[0], (B, S, DIM), jnp.float32), 'ws1': jax.random.normal(ks[1], (DIM, INTER), jnp.float32) * s, 'bs1': jnp.zeros((INTER,), jnp.float32), 'ws2': jax.random.normal(ks[2], (INTER, DIM), jnp.float32) * s, 'bs2': jnp.zeros((DIM,), jnp.float32), 'We1': jax.random.normal(ks[3], (E, DIM, INTER), jnp.float32) * s, 'Be1': jnp.zeros((E, INTER), jnp.float32), 'We2': jax.random.normal(ks[4], (E, INTER, DIM), jnp.float32) * s, 'Be2': jnp.zeros((E, DIM), jnp.float32), 'Wr': jax.random.normal(ks[5], (DIM, E), jnp.float32) * s, 'br': jnp.zeros((E,), jnp.float32)}
    _L3_ffn_all = _L3_ffn_setup()
    _L3_ffn_in = {k: v for k, v in _L3_ffn_all.items() if k in ('ws1', 'bs1', 'ws2', 'bs2', 'We1', 'Be1', 'We2', 'Be2', 'Wr', 'br')}
    del _L3_ffn_all
    return {'x': x, 'ctx_1024': ctx_1024, 'mask_1x1xSxS2_ik0': mask_1x1xSxS2_ik0, 'L0_attn_Wq': _L0_attn_in['Wq'], 'L0_attn_bq': _L0_attn_in['bq'], 'L0_attn_Wk': _L0_attn_in['Wk'], 'L0_attn_bk': _L0_attn_in['bk'], 'L0_attn_Wv': _L0_attn_in['Wv'], 'L0_attn_bv': _L0_attn_in['bv'], 'L0_attn_Wo': _L0_attn_in['Wo'], 'L0_attn_bo': _L0_attn_in['bo'], 'L0_xattn_Wk1': _L0_xattn_in['Wk1'], 'L0_xattn_Wv1': _L0_xattn_in['Wv1'], 'L0_xattn_Wq1': _L0_xattn_in['Wq1'], 'L0_xattn_Wo1': _L0_xattn_in['Wo1'], 'L0_xattn_bo1': _L0_xattn_in['bo1'], 'L0_xattn_Wk2': _L0_xattn_in['Wk2'], 'L0_xattn_Wv2': _L0_xattn_in['Wv2'], 'L0_xattn_Wq2': _L0_xattn_in['Wq2'], 'L0_xattn_Wo2': _L0_xattn_in['Wo2'], 'L0_xattn_bo2': _L0_xattn_in['bo2'], 'L0_xattn_Wf': _L0_xattn_in['Wf'], 'L0_xattn_bf': _L0_xattn_in['bf'], 'L0_xattn_g1': _L0_xattn_in['g1'], 'L0_xattn_b1': _L0_xattn_in['b1'], 'L0_xattn_g2': _L0_xattn_in['g2'], 'L0_xattn_b2': _L0_xattn_in['b2'], 'L0_xattn_g3': _L0_xattn_in['g3'], 'L0_xattn_b3': _L0_xattn_in['b3'], 'L0_ffn_w_int8': _L0_ffn_in['w_int8'], 'L0_ffn_weight_scale': _L0_ffn_in['weight_scale'], 'L0_ffn_bias': _L0_ffn_in['bias'], 'L1_attn_Wq': _L1_attn_in['Wq'], 'L1_attn_bq': _L1_attn_in['bq'], 'L1_attn_Wk': _L1_attn_in['Wk'], 'L1_attn_bk': _L1_attn_in['bk'], 'L1_attn_Wv': _L1_attn_in['Wv'], 'L1_attn_bv': _L1_attn_in['bv'], 'L1_attn_Wo': _L1_attn_in['Wo'], 'L1_attn_bo': _L1_attn_in['bo'], 'L1_xattn_Wq': _L1_xattn_in['Wq'], 'L1_xattn_bq': _L1_xattn_in['bq'], 'L1_xattn_Wk': _L1_xattn_in['Wk'], 'L1_xattn_bk': _L1_xattn_in['bk'], 'L1_xattn_Wv': _L1_xattn_in['Wv'], 'L1_xattn_bv': _L1_xattn_in['bv'], 'L1_xattn_Wo': _L1_xattn_in['Wo'], 'L1_xattn_bo': _L1_xattn_in['bo'], 'L1_ffn_Wr': _L1_ffn_in['Wr'], 'L1_ffn_br': _L1_ffn_in['br'], 'L1_ffn_W1': _L1_ffn_in['W1'], 'L1_ffn_b1': _L1_ffn_in['b1'], 'L1_ffn_W2': _L1_ffn_in['W2'], 'L1_ffn_b2': _L1_ffn_in['b2'], 'L2_attn_encoder_hidden_states': _L2_attn_in['encoder_hidden_states'], 'L2_attn_scorer_logits': _L2_attn_in['scorer_logits'], 'L2_attn_ln1_g': _L2_attn_in['ln1_g'], 'L2_attn_ln1_b': _L2_attn_in['ln1_b'], 'L2_attn_c_attn_w': _L2_attn_in['c_attn_w'], 'L2_attn_c_attn_b': _L2_attn_in['c_attn_b'], 'L2_attn_attn_proj_w': _L2_attn_in['attn_proj_w'], 'L2_attn_attn_proj_b': _L2_attn_in['attn_proj_b'], 'L2_attn_lnx_g': _L2_attn_in['lnx_g'], 'L2_attn_lnx_b': _L2_attn_in['lnx_b'], 'L2_attn_q_attn_w': _L2_attn_in['q_attn_w'], 'L2_attn_q_attn_b': _L2_attn_in['q_attn_b'], 'L2_attn_x_kv_w': _L2_attn_in['x_kv_w'], 'L2_attn_x_kv_b': _L2_attn_in['x_kv_b'], 'L2_attn_x_proj_w': _L2_attn_in['x_proj_w'], 'L2_attn_x_proj_b': _L2_attn_in['x_proj_b'], 'L2_attn_ln2_g': _L2_attn_in['ln2_g'], 'L2_attn_ln2_b': _L2_attn_in['ln2_b'], 'L2_attn_fc_w': _L2_attn_in['fc_w'], 'L2_attn_fc_b': _L2_attn_in['fc_b'], 'L2_attn_mlp_proj_w': _L2_attn_in['mlp_proj_w'], 'L2_attn_mlp_proj_b': _L2_attn_in['mlp_proj_b'], 'L2_xattn_Wq': _L2_xattn_in['Wq'], 'L2_xattn_bq': _L2_xattn_in['bq'], 'L2_xattn_Wk': _L2_xattn_in['Wk'], 'L2_xattn_bk': _L2_xattn_in['bk'], 'L2_xattn_Wv': _L2_xattn_in['Wv'], 'L2_xattn_bv': _L2_xattn_in['bv'], 'L2_xattn_Wo': _L2_xattn_in['Wo'], 'L2_xattn_bo': _L2_xattn_in['bo'], 'L2_ffn_Wr': _L2_ffn_in['Wr'], 'L2_ffn_br': _L2_ffn_in['br'], 'L2_ffn_W1': _L2_ffn_in['W1'], 'L2_ffn_b1': _L2_ffn_in['b1'], 'L2_ffn_W2': _L2_ffn_in['W2'], 'L2_ffn_b2': _L2_ffn_in['b2'], 'L3_attn_in_proj_weight': _L3_attn_in['in_proj_weight'], 'L3_attn_in_proj_bias': _L3_attn_in['in_proj_bias'], 'L3_attn_out_proj_weight': _L3_attn_in['out_proj_weight'], 'L3_attn_out_proj_bias': _L3_attn_in['out_proj_bias'], 'L3_xattn_Wq': _L3_xattn_in['Wq'], 'L3_xattn_bq': _L3_xattn_in['bq'], 'L3_xattn_Wk': _L3_xattn_in['Wk'], 'L3_xattn_bk': _L3_xattn_in['bk'], 'L3_xattn_Wv': _L3_xattn_in['Wv'], 'L3_xattn_bv': _L3_xattn_in['bv'], 'L3_xattn_Wo': _L3_xattn_in['Wo'], 'L3_xattn_bo': _L3_xattn_in['bo'], 'L3_ffn_ws1': _L3_ffn_in['ws1'], 'L3_ffn_bs1': _L3_ffn_in['bs1'], 'L3_ffn_ws2': _L3_ffn_in['ws2'], 'L3_ffn_bs2': _L3_ffn_in['bs2'], 'L3_ffn_We1': _L3_ffn_in['We1'], 'L3_ffn_Be1': _L3_ffn_in['Be1'], 'L3_ffn_We2': _L3_ffn_in['We2'], 'L3_ffn_Be2': _L3_ffn_in['Be2'], 'L3_ffn_Wr': _L3_ffn_in['Wr'], 'L3_ffn_br': _L3_ffn_in['br']}

def reference(x, ctx_1024, mask_1x1xSxS2_ik0, L0_attn_Wq, L0_attn_bq, L0_attn_Wk, L0_attn_bk, L0_attn_Wv, L0_attn_bv, L0_attn_Wo, L0_attn_bo, L0_xattn_Wk1, L0_xattn_Wv1, L0_xattn_Wq1, L0_xattn_Wo1, L0_xattn_bo1, L0_xattn_Wk2, L0_xattn_Wv2, L0_xattn_Wq2, L0_xattn_Wo2, L0_xattn_bo2, L0_xattn_Wf, L0_xattn_bf, L0_xattn_g1, L0_xattn_b1, L0_xattn_g2, L0_xattn_b2, L0_xattn_g3, L0_xattn_b3, L0_ffn_w_int8, L0_ffn_weight_scale, L0_ffn_bias, L1_attn_Wq, L1_attn_bq, L1_attn_Wk, L1_attn_bk, L1_attn_Wv, L1_attn_bv, L1_attn_Wo, L1_attn_bo, L1_xattn_Wq, L1_xattn_bq, L1_xattn_Wk, L1_xattn_bk, L1_xattn_Wv, L1_xattn_bv, L1_xattn_Wo, L1_xattn_bo, L1_ffn_Wr, L1_ffn_br, L1_ffn_W1, L1_ffn_b1, L1_ffn_W2, L1_ffn_b2, L2_attn_encoder_hidden_states, L2_attn_scorer_logits, L2_attn_ln1_g, L2_attn_ln1_b, L2_attn_c_attn_w, L2_attn_c_attn_b, L2_attn_attn_proj_w, L2_attn_attn_proj_b, L2_attn_lnx_g, L2_attn_lnx_b, L2_attn_q_attn_w, L2_attn_q_attn_b, L2_attn_x_kv_w, L2_attn_x_kv_b, L2_attn_x_proj_w, L2_attn_x_proj_b, L2_attn_ln2_g, L2_attn_ln2_b, L2_attn_fc_w, L2_attn_fc_b, L2_attn_mlp_proj_w, L2_attn_mlp_proj_b, L2_xattn_Wq, L2_xattn_bq, L2_xattn_Wk, L2_xattn_bk, L2_xattn_Wv, L2_xattn_bv, L2_xattn_Wo, L2_xattn_bo, L2_ffn_Wr, L2_ffn_br, L2_ffn_W1, L2_ffn_b1, L2_ffn_W2, L2_ffn_b2, L3_attn_in_proj_weight, L3_attn_in_proj_bias, L3_attn_out_proj_weight, L3_attn_out_proj_bias, L3_xattn_Wq, L3_xattn_bq, L3_xattn_Wk, L3_xattn_bk, L3_xattn_Wv, L3_xattn_bv, L3_xattn_Wo, L3_xattn_bo, L3_ffn_ws1, L3_ffn_bs1, L3_ffn_ws2, L3_ffn_bs2, L3_ffn_We1, L3_ffn_Be1, L3_ffn_We2, L3_ffn_Be2, L3_ffn_Wr, L3_ffn_br):
    import jax
    import jax.numpy as jnp

    def _L0_attn_ref(x, Wq, bq, Wk, bk, Wv, bv, Wo, bo):
        import jax, jax.numpy as jnp
        import numpy as np
        D_MODEL = 128
        NHEAD = 16
        D_HEAD = D_MODEL // NHEAD
        THETA = 10000.0

        def _apply_rope(Q, K):
            B, H, T, D = Q.shape
            qr, qi = (Q.reshape(B, H, T, D // 2, 2)[..., 0], Q.reshape(B, H, T, D // 2, 2)[..., 1])
            kr, ki = (K.reshape(B, H, T, D // 2, 2)[..., 0], K.reshape(B, H, T, D // 2, 2)[..., 1])
            freqs = jnp.arange(D // 2, dtype=jnp.float32) * (1.0 / THETA)
            angles = jnp.arange(T, dtype=jnp.float32)[:, None] * freqs[None, :]
            cos = jnp.cos(angles)[None, None]
            sin = jnp.sin(angles)[None, None]
            qr2 = qr * cos - qi * sin
            qi2 = qr * sin + qi * cos
            kr2 = kr * cos - ki * sin
            ki2 = kr * sin + ki * cos
            Q2 = jnp.stack([qr2, qi2], axis=-1).reshape(B, H, T, D)
            K2 = jnp.stack([kr2, ki2], axis=-1).reshape(B, H, T, D)
            return (Q2, K2)
        B, T, d_model = x.shape
        Q = x @ Wq.T + bq
        K = x @ Wk.T + bk
        V = x @ Wv.T + bv
        Q = Q.reshape(B, T, NHEAD, D_HEAD).transpose(0, 2, 1, 3)
        K = K.reshape(B, T, NHEAD, D_HEAD).transpose(0, 2, 1, 3)
        V = V.reshape(B, T, NHEAD, D_HEAD).transpose(0, 2, 1, 3)
        Q, K = _apply_rope(Q, K)
        scores = jnp.einsum('bhqd,bhkd->bhqk', Q, K) / jnp.sqrt(jnp.float32(D_HEAD))
        attn = jax.nn.softmax(scores, axis=-1)
        out = jnp.einsum('bhqk,bhkd->bhqd', attn, V)
        out = out.transpose(0, 2, 1, 3).reshape(B, T, d_model)
        return out @ Wo.T + bo

    def _L0_xattn_ref(inputs, context_seq, Wk1, Wv1, Wq1, Wo1, bo1, Wk2, Wv2, Wq2, Wo2, bo2, Wf, bf, g1, b1, g2, b2, g3, b3):
        import jax, jax.numpy as jnp
        import numpy as np
        B, S, SC, E, H = (2, 256, 256, 128, 16)
        D = E // H
        EPS = 1e-06

        def _layernorm(x, g, b):
            m = jnp.mean(x, axis=-1, keepdims=True)
            v = jnp.mean((x - m) ** 2, axis=-1, keepdims=True)
            return (x - m) / jnp.sqrt(v + EPS) * g + b

        def _mha(xk, xv, xq, Wk, Wv, Wq, Wo, bo, masked):
            K = jnp.einsum('bse,hed->bhsd', xk, Wk)
            V = jnp.einsum('bse,hed->bhsd', xv, Wv)
            Q = jnp.einsum('bqe,hed->bhqd', xq, Wq)
            scores = jnp.einsum('bhqd,bhkd->bhqk', Q, K)
            sk = xk.shape[1]
            if masked:
                causal = jnp.triu(jnp.ones((xq.shape[1], sk), dtype=bool), k=1)
                scores = jnp.where(causal, -jnp.inf, scores)
            att = jax.nn.softmax(scores / jnp.sqrt(jnp.asarray(sk, scores.dtype)), axis=-1)
            out = jnp.einsum('bhqk,bhkd->bhqd', att, V)
            out = out.transpose(0, 2, 1, 3).reshape(out.shape[0], out.shape[2], -1)
            return jax.nn.relu(out @ Wo + bo)
        a = _mha(inputs, inputs, inputs, Wk1, Wv1, Wq1, Wo1, bo1, masked=True)
        a = _layernorm(inputs + a, g1, b1)
        c = _mha(context_seq, context_seq, a, Wk2, Wv2, Wq2, Wo2, bo2, masked=False)
        c = _layernorm(c + c, g2, b2)
        f = jax.nn.relu(c @ Wf + bf)
        return _layernorm(c + f, g3, b3)

    def _L0_ffn_ref(x, w_int8, weight_scale, bias):
        import jax, jax.numpy as jnp
        import numpy as np
        EPS_RMS = 1e-06
        EPS_ACT = 1e-05

        def simple_rms_norm(x):
            ms = jnp.mean(jnp.square(x), axis=-1, keepdims=True)
            return x * jax.lax.rsqrt(ms + EPS_RMS)

        def activation_quant(x):
            absmax = jnp.max(jnp.abs(jax.lax.stop_gradient(x)), axis=-1, keepdims=True)
            scale = 127.0 / jnp.clip(absmax, EPS_ACT, None)
            q = jnp.clip(jnp.round(x * scale), -128.0, 127.0) / scale
            return x + jax.lax.stop_gradient(q - x)
        w_deq = w_int8.astype(jnp.float32) * (1.0 / weight_scale) * weight_scale ** 0 * weight_scale
        w_deq = w_int8.astype(jnp.float32) * weight_scale
        x_norm = simple_rms_norm(x)
        x_q = activation_quant(x_norm)
        return jnp.einsum('bsd,od->bso', x_q, w_deq) + bias

    def _L1_attn_ref(x, Wq, bq, Wk, bk, Wv, bv, Wo, bo):
        import jax, jax.numpy as jnp
        import numpy as np
        DIM = 128
        NUM_HEADS = 16
        HEAD_DIM = DIM // NUM_HEADS
        TAU = 1.0
        LAMBDA_JUMP = 0.6
        LAMBDA_LOCAL = 0.4
        MIN_ENTROPY = 0.5
        WINDOW = 3
        EPS = 1e-10

        def local_diffusion_kernel(seq_len, strength, window=WINDOW):
            i = jnp.arange(seq_len)
            d = i[:, None] - i[None, :]
            k = jnp.where(jnp.abs(d) <= window, jnp.exp(-d.astype(jnp.float32) ** 2 / (2.0 * strength ** 2)), 0.0)
            return k / (k.sum(axis=-1, keepdims=True) + EPS)
        B, S, D = x.shape
        H, hd = (NUM_HEADS, HEAD_DIM)
        Q = (x @ Wq.T + bq).reshape(B, S, H, hd).transpose(0, 2, 1, 3)
        K = (x @ Wk.T + bk).reshape(B, S, H, hd).transpose(0, 2, 1, 3)
        V = (x @ Wv.T + bv).reshape(B, S, H, hd).transpose(0, 2, 1, 3)
        scores = jnp.einsum('bhqd,bhkd->bhqk', Q, K) / (TAU * np.sqrt(hd).astype(np.float32))
        A = jax.nn.softmax(scores, axis=-1)
        entropy = -jnp.sum(A * jnp.log(A + EPS), axis=-1, keepdims=True)
        stable = jax.lax.stop_gradient((entropy >= MIN_ENTROPY).astype(A.dtype))
        A = stable * A + (1.0 - stable) * jax.lax.stop_gradient(A)
        L = local_diffusion_kernel(S, LAMBDA_LOCAL)
        A_stable = LAMBDA_JUMP * A + (1.0 - LAMBDA_JUMP) * L[None, None, :, :]
        out = jnp.einsum('bhqk,bhkd->bhqd', A_stable, V)
        out = out.transpose(0, 2, 1, 3).reshape(B, S, D)
        return out @ Wo.T + bo

    def _L1_xattn_ref(query, key, value, mask, Wq, bq, Wk, bk, Wv, bv, Wo, bo):
        import jax, jax.numpy as jnp
        import numpy as np
        NEG_INF = -10000000000.0
        D_MODEL = 128
        NUM_HEADS = 16
        HEAD_DIM = D_MODEL // NUM_HEADS
        B, S = (2, 256)

        def _split_heads(x):
            b, s, _ = x.shape
            return x.reshape(b, s, NUM_HEADS, HEAD_DIM).transpose(0, 2, 1, 3)
        q = _split_heads(query @ Wq.T + bq)
        k = _split_heads(key @ Wk.T + bk)
        v = _split_heads(value @ Wv.T + bv)
        scale = 1.0 / jnp.sqrt(jnp.float32(HEAD_DIM))
        scores = jnp.einsum('bhqd,bhkd->bhqk', q, k) * scale
        scores = jnp.where(mask == 0, NEG_INF, scores)
        probs = jax.nn.softmax(scores, axis=-1)
        out = jnp.einsum('bhqk,bhkd->bhqd', probs, v)
        out = out.transpose(0, 2, 1, 3).reshape(query.shape[0], -1, D_MODEL)
        return out @ Wo.T + bo

    def _L1_ffn_ref(x, Wr, br, W1, b1, W2, b2):
        import jax, jax.numpy as jnp
        import numpy as np
        H, E, DFF = (128, 8, 512)
        B, S, Hd = x.shape
        n_exp = W1.shape[0]
        xt = x.reshape(-1, Hd)
        logits = xt @ Wr + br
        probs = jax.nn.softmax(logits, axis=-1)
        gate = jnp.max(probs, axis=-1)
        idx = jnp.argmax(probs, axis=-1)
        h1 = jnp.maximum(jnp.einsum('th,ehf->etf', xt, W1) + b1[:, None, :], 0.0)
        ye = jnp.einsum('etf,efh->eth', h1, W2) + b2[:, None, :]
        onehot = jax.nn.one_hot(idx, n_exp, dtype=xt.dtype)
        y = jnp.einsum('te,eth->th', onehot, ye) * gate[:, None]
        return y.reshape(B, S, Hd)

    def _L2_attn_ref(hidden_states, encoder_hidden_states, scorer_logits, ln1_g, ln1_b, c_attn_w, c_attn_b, attn_proj_w, attn_proj_b, lnx_g, lnx_b, q_attn_w, q_attn_b, x_kv_w, x_kv_b, x_proj_w, x_proj_b, ln2_g, ln2_b, fc_w, fc_b, mlp_proj_w, mlp_proj_b):
        import jax, jax.numpy as jnp
        import numpy as np
        B, S, SE, H, NH = (1, 256, 256, 128, 16)
        HD = H // NH
        INNER = 4 * H
        EPS = 1e-05

        def layer_norm(x, g, b):
            mu = jnp.mean(x, axis=-1, keepdims=True)
            var = jnp.mean(jnp.square(x - mu), axis=-1, keepdims=True)
            return (x - mu) * jax.lax.rsqrt(var + EPS) * g + b

        def split_heads(x):
            b, t, _ = x.shape
            return x.reshape(b, t, NH, HD).transpose(0, 2, 1, 3)

        def merge_heads(x):
            b, nh, t, hd = x.shape
            return x.transpose(0, 2, 1, 3).reshape(b, t, nh * hd)

        def _attn_core(q, k, v, extra_bias=None, causal_bool=False, tril_diag2_additive=False):
            w = jnp.einsum('bhqd,bhkd->bhqk', q, k) / jnp.sqrt(jnp.asarray(HD, q.dtype))
            ql, kl = (q.shape[-2], k.shape[-2])
            neg = jnp.finfo(w.dtype).min
            if causal_bool:
                mask = jnp.tril(jnp.ones((ql, kl), bool))
                w = jnp.where(mask[None, None], w, neg)
            if tril_diag2_additive:
                cm = jnp.tril(jnp.ones((ql, kl), w.dtype), k=2)
                w = w + jnp.where(cm == 0, neg, jnp.zeros((), w.dtype))[None, None]
            if extra_bias is not None:
                w = w + extra_bias[:, None, None, :]
            w = jax.nn.softmax(w, axis=-1)
            return jnp.einsum('bhqk,bhkd->bhqd', w, v)
        residual = hidden_states
        x = layer_norm(hidden_states, ln1_g, ln1_b)
        qkv = x @ c_attn_w + c_attn_b
        q, k, v = jnp.split(qkv, 3, axis=-1)
        a = _attn_core(split_heads(q), split_heads(k), split_heads(v), causal_bool=True)
        a = merge_heads(a) @ attn_proj_w + attn_proj_b
        hidden_states = a + residual
        residual = hidden_states
        x = layer_norm(hidden_states, lnx_g, lnx_b)
        q = x @ q_attn_w + q_attn_b
        kv = encoder_hidden_states @ x_kv_w + x_kv_b
        k, v = jnp.split(kv, 2, axis=-1)
        a = _attn_core(split_heads(q), split_heads(k), split_heads(v), extra_bias=scorer_logits, tril_diag2_additive=True)
        a = merge_heads(a) @ x_proj_w + x_proj_b
        hidden_states = residual + a
        residual = hidden_states
        x = layer_norm(hidden_states, ln2_g, ln2_b)
        h = jax.nn.gelu(x @ fc_w + fc_b, approximate=True)
        hidden_states = residual + (h @ mlp_proj_w + mlp_proj_b)
        return hidden_states

    def _L2_xattn_ref(query_states, key_value_states, Wq, bq, Wk, bk, Wv, bv, Wo, bo):
        import jax, jax.numpy as jnp
        import numpy as np
        HIDDEN = 128
        NUM_HEADS = 16
        HEAD_DIM = HIDDEN // NUM_HEADS
        SCALE = 1.0 / float(np.sqrt(HEAD_DIM))
        B, SQ, _ = query_states.shape
        _, SKV, _ = key_value_states.shape
        q = query_states @ Wq.T + bq
        k = key_value_states @ Wk.T + bk
        v = key_value_states @ Wv.T + bv
        q = q.reshape(B, SQ, NUM_HEADS, HEAD_DIM).transpose(0, 2, 1, 3) * SCALE
        k = k.reshape(B, SKV, NUM_HEADS, HEAD_DIM).transpose(0, 2, 1, 3)
        v = v.reshape(B, SKV, NUM_HEADS, HEAD_DIM).transpose(0, 2, 1, 3)
        scores = jnp.einsum('bhqd,bhkd->bhqk', q, k)
        attn = jax.nn.softmax(scores, axis=-1)
        ctx = jnp.einsum('bhqk,bhkd->bhqd', attn, v)
        ctx = ctx.transpose(0, 2, 1, 3).reshape(B, SQ, HIDDEN)
        return ctx @ Wo.T + bo

    def _L2_ffn_ref(tensor, Wr, br, W1, b1, W2, b2):
        import jax, jax.numpy as jnp
        import numpy as np
        D_MODEL = 128
        D_HIDDEN = 512
        NUM_BANKS = 16
        NUM_SELECTED = 2
        logits = jnp.einsum('bsd,de->bse', tensor, Wr) + br
        probs = jax.nn.softmax(logits, axis=-1)
        topv, topi = jax.lax.top_k(probs, NUM_SELECTED)
        gate = jnp.sum(jax.nn.one_hot(topi, NUM_BANKS, dtype=tensor.dtype) * topv[..., None], axis=-2)
        h = jax.nn.relu(jnp.einsum('bsd,edh->bseh', tensor, W1) + b1)
        y = jnp.einsum('bseh,ehm->bsem', h, W2) + b2
        out = jnp.einsum('bse,bsem->bsm', gate, y)
        return out

    def _L3_attn_ref(src, in_proj_weight, in_proj_bias, out_proj_weight, out_proj_bias):
        import jax, jax.numpy as jnp
        import numpy as np
        S, B, F = (256, 2, 128)
        H, D = (16, 64)
        P = H * D
        s, b, f = src.shape
        h, d = (H, D)
        qkv = jnp.einsum('sbf,pf->sbp', src, in_proj_weight) + in_proj_bias
        q, k, v = jnp.split(qkv, 3, axis=-1)

        def to_heads(x):
            return jnp.swapaxes(x.reshape(s, b * h, d), 0, 1)
        q = to_heads(q) / np.sqrt(d)
        k = to_heads(k)
        v = to_heads(v)
        attn = jnp.einsum('nsd,ntd->nst', q, k)
        attn = jax.nn.softmax(attn, axis=-1)
        out = jnp.einsum('nst,ntd->nsd', attn, v)
        out = jnp.swapaxes(out, 0, 1).reshape(s * b, h * d)
        out = out @ out_proj_weight.T + out_proj_bias
        return out.reshape(s, b, f)

    def _L3_xattn_ref(query, key, value, Wq, bq, Wk, bk, Wv, bv, Wo, bo):
        import jax, jax.numpy as jnp
        import numpy as np
        D_MODEL = 128
        NUM_HEADS = 16
        HEAD_DIM = D_MODEL // NUM_HEADS
        SCALE = HEAD_DIM ** (-0.5)
        B, S = (2, 256)
        b, sq, _ = query.shape
        skv = key.shape[1]
        q = (query @ Wq + bq).reshape(b, sq, NUM_HEADS, HEAD_DIM).transpose(0, 2, 1, 3)
        k = (key @ Wk + bk).reshape(b, skv, NUM_HEADS, HEAD_DIM).transpose(0, 2, 1, 3)
        v = (value @ Wv + bv).reshape(b, skv, NUM_HEADS, HEAD_DIM).transpose(0, 2, 1, 3)
        scores = jnp.einsum('bhqd,bhkd->bhqk', q, k) * SCALE
        attn = jax.nn.softmax(scores, axis=-1)
        out = jnp.einsum('bhqk,bhkd->bhqd', attn, v)
        out = out.transpose(0, 2, 1, 3).reshape(b, sq, D_MODEL)
        return out @ Wo + bo

    def _L3_ffn_ref(x, ws1, bs1, ws2, bs2, We1, Be1, We2, Be2, Wr, br):
        import jax, jax.numpy as jnp
        import numpy as np
        B, S, DIM = (4, 256, 128)
        INTER = int(int(DIM * 4) * 0.25)
        E = 32 - 1
        K = 4 - 1

        def _gelu(t):
            return jax.nn.gelu(t, approximate=False)
        shared = _gelu(x @ ws1 + bs1) @ ws2 + bs2
        aff = jax.nn.softmax(x @ Wr + br, axis=-1)
        vals, idx = jax.lax.top_k(aff, K)
        gates = jnp.sum(jax.nn.one_hot(idx, E, dtype=x.dtype) * vals[..., None], axis=-2)
        gates_e = jnp.moveaxis(gates, -1, 0)

        def step(acc, p):
            W1, B1, W2, B2, g = p
            h = _gelu(x @ W1 + B1)
            return (acc + g[..., None] * (h @ W2 + B2), None)
        routed, _ = jax.lax.scan(step, jnp.zeros_like(x), (We1, Be1, We2, Be2, gates_e))
        return shared + routed + x
    x = _layernorm(x + _L0_attn_ref(x, L0_attn_Wq, L0_attn_bq, L0_attn_Wk, L0_attn_bk, L0_attn_Wv, L0_attn_bv, L0_attn_Wo, L0_attn_bo), axis=-1)
    x = _layernorm(x + _L0_xattn_ref(x, ctx_1024, L0_xattn_Wk1, L0_xattn_Wv1, L0_xattn_Wq1, L0_xattn_Wo1, L0_xattn_bo1, L0_xattn_Wk2, L0_xattn_Wv2, L0_xattn_Wq2, L0_xattn_Wo2, L0_xattn_bo2, L0_xattn_Wf, L0_xattn_bf, L0_xattn_g1, L0_xattn_b1, L0_xattn_g2, L0_xattn_b2, L0_xattn_g3, L0_xattn_b3), axis=-1)
    x = _layernorm(x + _L0_ffn_ref(x, L0_ffn_w_int8, L0_ffn_weight_scale, L0_ffn_bias), axis=-1)
    x = _layernorm(x + _L1_attn_ref(x, L1_attn_Wq, L1_attn_bq, L1_attn_Wk, L1_attn_bk, L1_attn_Wv, L1_attn_bv, L1_attn_Wo, L1_attn_bo), axis=-1)
    x = _layernorm(x + _L1_xattn_ref(x, ctx_1024, ctx_1024, mask_1x1xSxS2_ik0, L1_xattn_Wq, L1_xattn_bq, L1_xattn_Wk, L1_xattn_bk, L1_xattn_Wv, L1_xattn_bv, L1_xattn_Wo, L1_xattn_bo), axis=-1)
    x = _layernorm(x + _L1_ffn_ref(x, L1_ffn_Wr, L1_ffn_br, L1_ffn_W1, L1_ffn_b1, L1_ffn_W2, L1_ffn_b2), axis=-1)
    x = _layernorm(x + _L2_attn_ref(x, L2_attn_encoder_hidden_states, L2_attn_scorer_logits, L2_attn_ln1_g, L2_attn_ln1_b, L2_attn_c_attn_w, L2_attn_c_attn_b, L2_attn_attn_proj_w, L2_attn_attn_proj_b, L2_attn_lnx_g, L2_attn_lnx_b, L2_attn_q_attn_w, L2_attn_q_attn_b, L2_attn_x_kv_w, L2_attn_x_kv_b, L2_attn_x_proj_w, L2_attn_x_proj_b, L2_attn_ln2_g, L2_attn_ln2_b, L2_attn_fc_w, L2_attn_fc_b, L2_attn_mlp_proj_w, L2_attn_mlp_proj_b), axis=-1)
    x = _layernorm(x + _L2_xattn_ref(x, ctx_1024, L2_xattn_Wq, L2_xattn_bq, L2_xattn_Wk, L2_xattn_bk, L2_xattn_Wv, L2_xattn_bv, L2_xattn_Wo, L2_xattn_bo), axis=-1)
    x = _layernorm(x + _L2_ffn_ref(x, L2_ffn_Wr, L2_ffn_br, L2_ffn_W1, L2_ffn_b1, L2_ffn_W2, L2_ffn_b2), axis=-1)
    x = _layernorm(x + _L3_attn_ref(x, L3_attn_in_proj_weight, L3_attn_in_proj_bias, L3_attn_out_proj_weight, L3_attn_out_proj_bias), axis=-1)
    x = _layernorm(x + _L3_xattn_ref(x, ctx_1024, ctx_1024, L3_xattn_Wq, L3_xattn_bq, L3_xattn_Wk, L3_xattn_bk, L3_xattn_Wv, L3_xattn_bv, L3_xattn_Wo, L3_xattn_bo), axis=-1)
    x = _layernorm(x + _L3_ffn_ref(x, L3_ffn_ws1, L3_ffn_bs1, L3_ffn_ws2, L3_ffn_bs2, L3_ffn_We1, L3_ffn_Be1, L3_ffn_We2, L3_ffn_Be2, L3_ffn_Wr, L3_ffn_br), axis=-1)
    return x

_drawn_inputs = setup_inputs


def setup_inputs(seed=0):
    import zlib

    import numpy as np

    out = dict(_drawn_inputs(seed))
    spreads = {'L0_attn_bq': (0.0, 0.341),
     'L0_attn_bk': (0.0, 0.8),
     'L0_attn_bv': (0.0, 0.1),
     'L0_attn_bo': (0.0, 0.1),
     'L0_xattn_bo1': (0.0, 0.8),
     'L0_xattn_bo2': (0.0, 0.1),
     'L0_xattn_bf': (0.0, 0.1),
     'L0_xattn_g1': (1.0, 0.6),
     'L0_xattn_b1': (0.0, 0.8),
     'L0_xattn_g2': (1.0, 0.2),
     'L0_xattn_b2': (0.0, 0.1),
     'L0_xattn_g3': (1.0, 0.2),
     'L0_xattn_b3': (0.0, 0.1),
     'L1_ffn_br': (0.0, 0.1),
     'L1_ffn_b1': (0.0, 0.282),
     'L1_ffn_b2': (0.0, 0.1),
     'L2_attn_ln1_g': (1.0, 0.6),
     'L2_attn_ln1_b': (0.0, 0.8),
     'L2_attn_c_attn_b': (0.0, 0.765),
     'L2_attn_attn_proj_b': (0.0, 0.1),
     'L2_attn_lnx_g': (1.0, 0.6),
     'L2_attn_lnx_b': (0.0, 0.8),
     'L2_attn_q_attn_b': (0.0, 0.8),
     'L2_attn_x_kv_b': (0.0, 0.71),
     'L2_attn_x_proj_b': (0.0, 0.1),
     'L2_attn_ln2_g': (1.0, 0.6),
     'L2_attn_ln2_b': (0.0, 0.8),
     'L2_attn_fc_b': (0.0, 0.682),
     'L2_attn_mlp_proj_b': (0.0, 0.1),
     'L2_xattn_bq': (0.0, 0.8),
     'L2_xattn_bk': (0.0, 0.8),
     'L2_xattn_bv': (0.0, 0.358),
     'L2_xattn_bo': (0.0, 0.1),
     'L2_ffn_br': (0.0, 0.73),
     'L2_ffn_b1': (0.0, 0.8),
     'L2_ffn_b2': (0.0, 0.707),
     'L3_attn_in_proj_bias': (0.0, 0.1),
     'L3_attn_out_proj_bias': (0.0, 0.1),
     'L3_xattn_bq': (0.0, 0.295),
     'L3_xattn_bk': (0.0, 0.8),
     'L3_xattn_bv': (0.0, 0.1),
     'L3_xattn_bo': (0.0, 0.1),
     'L3_ffn_bs1': (0.0, 0.8),
     'L3_ffn_bs2': (0.0, 0.1),
     'L3_ffn_Be1': (0.0, 0.8),
     'L3_ffn_Be2': (0.0, 0.8),
     'L3_ffn_br': (0.0, 0.8)}
    factors = {'L0_xattn_Wk1': 8.0,
     'L0_xattn_Wv1': 8.0,
     'L0_xattn_Wq1': 8.0,
     'L0_xattn_Wo1': 8.0,
     'L0_xattn_Wk2': 4.655,
     'L0_xattn_Wq2': 5.442,
     'L0_ffn_bias': 8.0,
     'L1_attn_Wq': 8.0,
     'L1_attn_bq': 8.0,
     'L1_attn_Wk': 8.0,
     'L1_attn_bk': 8.0,
     'L1_attn_bv': 7.833,
     'L1_xattn_bk': 8.0,
     'L2_attn_encoder_hidden_states': 8.0,
     'L2_attn_scorer_logits': 8.0,
     'L2_attn_c_attn_w': 2.812,
     'L2_attn_q_attn_w': 8.0,
     'L2_attn_x_kv_w': 8.0,
     'L2_attn_x_proj_w': 5.097,
     'L2_xattn_Wq': 8.0,
     'L2_xattn_Wk': 8.0,
     'L2_ffn_Wr': 4.231,
     'L2_ffn_W1': 8.0,
     'L2_ffn_W2': 6.81,
     'L3_ffn_ws1': 4.073,
     'L3_ffn_ws2': 3.987,
     'L3_ffn_We1': 8.0,
     'L3_ffn_We2': 8.0,
     'L3_ffn_Wr': 8.0}
    for name, (base, spread) in spreads.items():
        noise = np.random.default_rng([zlib.crc32(name.encode()), seed]).standard_normal(out[name].shape)
        drawn = base * np.exp(spread * noise) if base else spread * noise
        out[name] = jnp.asarray(drawn.astype(out[name].dtype))
    for name, factor in factors.items():
        out[name] = (out[name] * factor).astype(out[name].dtype)
    return out
```

```python
from contextlib import ExitStack

import numpy as np

import concourse.bass as bass
from concourse import mybir

F32 = mybir.dt.float32
BF16 = mybir.dt.bfloat16
I32 = mybir.dt.int32
ALU = mybir.AluOpType
ACT = mybir.ActivationFunctionType
AX_X = mybir.AxisListType.X

P = 128
B, S, D = 4, 512, 128
QT = S // P
U = 2
H, DH = 16, D // 16
SC = 77
SE = 256
NB = 6
R_BIAS = NB * DH
R_MAX = R_BIAS + 3
R_END = R_MAX + 2
HG = 4
MASKED = -(2.0 ** 100)
F1, FT1 = 512, 4
E1, E2, E3 = 8, 16, 32
K1, K2, K3 = 1, 2, 3
LH, LD = 16, 64
LP = LH * LD
G3 = P // B
U3 = 4

BAND = [(kt, qt) for qt in range(QT) for kt in range(max(qt - 1, 0), min(qt + 2, QT))]

PACKED = (
    [("ident", P), ("rot", P), ("cos", S), ("sin", S), ("causal_q", P), ("causal_k", P), ("tril2_q", P),
     ("tril2_k", P), ("tril2b_q", P), ("tril2b_k", P), ("same_q", 4 * P), ("band", len(BAND) * P)]
    + [(f"{n}_{w}", D) for n in ("L0a", "L0s", "L0c", "L1a", "L1c", "L2s", "L2c", "L2x", "L3c")
       for w in ("wq", "wk", "wv", "wo")]
    + [(f"{n}_{w}", 1) for n in ("L0a", "L1a", "L1c", "L2s", "L2c", "L2x", "L3c") for w in ("bq", "bk")]
    + [("wf", D), ("g1", 1), ("b1", 1), ("g2", D), ("b2", D), ("g3", D), ("b3", D), ("wscale", 1)]
    + [(f"{n}_{w}", 1) for n in ("ln1", "lnx", "ln2") for w in ("g", "b")]
    + [("fc", F1), ("fc_b", FT1), ("mlp", FT1 * D), ("enc", SE)]
    + [("wr1", E1), ("wr2", E2), ("wr3", E3 - 1), ("e1_b1", E1 * FT1), ("e2_b1", E2 * FT1), ("e3_b1", E3)]
    + [("l3_bq", LP // P), ("l3_bk", LP // P)]
    + [("iota", 32)]
)
ROWS = (
    [(f"{n}_bv", D) for n in ("L0a", "L1a", "L1c", "L2s", "L2c", "L2x", "L3c")]
    + [(f"{n}_bo", D) for n in ("L0a", "L0s", "L0c", "L1a", "L1c", "L2s", "L2c", "L2x", "L3c")]
    + [("bf", D), ("q8_b", D), ("mlp_b", D), ("br1", E1), ("br2", E2), ("br3", E3 - 1), ("scorer", SE),
       ("l3_bo", D)]
)


def offsets(names):
    at, out = 0, {}
    for name, width in names:
        out[name] = (at, width)
        at += width
    return out, at


PACK_AT, PACK_W = offsets(PACKED)
ROW_AT, ROW_W = offsets(ROWS)


def since(eng, sem, n):
    if n > 0:
        eng.wait_ge(sem, n)


class Own:

    def __init__(self, eng, sem):
        self.eng, self.sem, self.n = eng, sem, 0

    def mark(self, ins):
        ins.then_inc(self.sem, 1)
        self.n += 1

    def wait(self):
        since(self.eng, self.sem, self.n)


class Stage:

    def __init__(self, nc, *names):
        self.nc, self.names = nc, names

    def __enter__(self):
        self.ctx = ExitStack()
        self.sems = [self.ctx.enter_context(self.nc.semaphore(n)) for n in self.names]
        self.block_ctx = ExitStack()
        self.block = self.block_ctx.enter_context(self.nc.Block())
        return self.block, *self.sems

    def __exit__(self, *e):
        self.block_ctx.__exit__(*e)
        if e[0] is None:
            numbers = sorted(s.num for s in self.sems)
            starts = [n for n in numbers if n - 1 not in numbers]
            ends = [n for n in numbers if n + 1 not in numbers]
            for first, last in zip(starts, ends):
                self.nc.gpsimd.sem_clear(range(first, last + 1))
            self.nc.all_engine_barrier()
        self.ctx.__exit__(*e)
        return False


class Attention:

    def __init__(self, name, q, kv, nk, scale, post, masks=None, rope=False, bias=None, local=False,
                 zero_bias_rows=False):
        self.name, self.q, self.kv, self.nk, self.scale, self.post = name, q, kv, nk, scale, post
        self.masks, self.rope, self.bias, self.local = masks, rope, bias, local
        self.zero_bias_rows = zero_bias_rows
        self.kn = min(nk, P)
        self.kt = (nk + P - 1) // P
        causal = masks == "causal"
        self.keys_of = [(t + 1) * P if causal else nk for t in range(QT)]
        self.first_q = [k * P if causal else 0 for k in range(self.kt)]
        self.kts_of = [range(t + 1) if causal else range(self.kt) for t in range(QT)]


def build(nc, io):
    ctx = ExitStack()
    with ctx:
        def sb(name, shape, dt=F32):
            return ctx.enter_context(nc.sbuf_tensor(name, shape, dt))

        def ps(name, shape):
            return ctx.enter_context(nc.psum_tensor(name, shape, F32))

        pack = sb("pack", [P, PACK_W])
        rows = sb("rows", [1, ROW_W])

        def col(name, a=0, b=None):
            at, width = PACK_AT[name]
            return pack[:, at + a:at + (width if b is None else b)]

        def row(name):
            at, width = ROW_AT[name]
            return rows[0:1, at:at + width]

        ident = col("ident")
        ones = sb("ones", [1, P])
        ident_bf = sb("ident_bf", [P, P], BF16)
        masks_bf = sb("masks_bf", [P, 6 * P], BF16)
        same_bf = sb("same_bf", [P, 4 * P], BF16)
        ctx_mask_q = sb("ctx_mask_q", [P, QT, SC], BF16)
        ctx_mask_k = sb("ctx_mask_k", [SC, S], BF16)
        zeros_bf = sb("zeros_bf", [3, S], BF16)
        bias_parts = sb("bias_parts", [1, 3, SE], BF16)
        w_q8 = sb("w_q8", [P, D])

        x_all = sb("x_all", [P, B, S])
        xt = sb("xt", [P, U, QT, D])
        xT = sb("xT", [P, U, S])
        nT = sb("nT", [P, U, S])
        yt = sb("yt", [P, U, QT, D])
        hres = sb("hres", [P, U, QT, D])
        ctxT = sb("ctxT", [P, U, SC])

        q_stack = sb("q_stack", [P, U, H // 2, S], BF16)
        k_stack = sb("k_stack", [P, U, H // 2, S], BF16)
        work = sb("work", [P, 4, S])
        q_full, k_full, q_tmp, k_tmp = (work[:, n, :] for n in range(4))
        q_parts = sb("q_parts", [P, 3, S], BF16)
        k_parts = sb("k_parts", [P, 3, S], BF16)
        values = sb("values", [P, U, QT, H, 32])
        o_raw = sb("o_raw", [P, S])
        probs = sb("probs", [P, 2, QT, S])
        maxima = sb("maxima", [P, U, QT, H])
        max_rows = sb("max_rows", [HG, 2, 2, S], BF16)
        recip = sb("recip", [P, QT * HG])
        ot = sb("ot", [P, QT, D])
        oT = sb("oT", [P, S])
        stats = sb("stats", [P, QT, 6])
        mean_var = sb("mean_var", [P, QT, 2])
        rstd = sb("rstd", [P, QT])
        var_eps = sb("var_eps", [P, QT])
        newton = sb("newton", [P, QT])

        logits = sb("logits", [P, QT, 32])
        rprobs = sb("rprobs", [P, QT, 32])
        pick = sb("pick", [P, QT, 32])
        gates = sb("gates", [P, U, QT, 32])
        r1 = sb("r1", [P, QT])
        gatesT = sb("gatesT", [32, U, S])
        e_b2 = sb("e_b2", [32, 3, D])
        experts = sb("experts", [P, 4, 2 * F1])

        ring = experts[:].rearrange("p r n -> p (r n)")
        in_w = ring[:, 0:3 * LP]
        out_w = ring[:, 3 * LP:4 * LP].rearrange("p (j d) -> p j d", d=D)

        psM = ps("psM", [P, 2, 512])
        psE = ps("psE", [P, 2, 512])
        psO = ps("psO", [P, 2, 512])
        psA = ps("psA", [P, 512])
        psB = ps("psB", [P, 512])

        loads = ctx.enter_context(nc.semaphore("loads"))
        loads3 = ctx.enter_context(nc.semaphore("loads3"))

        mask_at = {n: masks_bf[:, i * P:(i + 1) * P] for i, n in enumerate(
            ("causal_q", "causal_k", "tril2_q", "tril2_k", "tril2b_q", "tril2b_k"))}

        N_LOADS = 4
        with Stage(nc, "cast", "zeroed", "own") as (block, cast, zeroed, own):
            mask_q_i = probs[:, 0, 0, 0:QT * SC].bitcast(I32)
            mask_k_i = probs[0:SC, 0, 1, :].bitcast(I32)
            w_q8_i = probs[:, 0, 2, 0:D].bitcast(I32)

            @block.sync
            def _(sp):
                sp.dma_start(pack[:], io["pack"]).then_inc(loads, 16)
                sp.dma_start(rows[:], io["rows"]).then_inc(loads, 16)
                sp.dma_start(mask_q_i, io["mask_q"]).then_inc(loads, 16)
                sp.dma_start(mask_k_i, io["mask_k"]).then_inc(loads, 16)
                sp.dma_start(w_q8_i, io["w_q8"]).then_inc(loads, 16)
                sp.dma_start(e_b2[:], io["e_b2"]).then_inc(loads, 16)
                sp.wait_ge(cast, 3)
                for hb in range(2):
                    for u in range(U):
                        sp.dma_start(k_stack[64 * hb + R_BIAS:64 * hb + R_MAX, u],
                                     zeros_bf[:].unsqueeze(1).to_broadcast([3, H // 2, S])).then_inc(zeroed, 16)
                sp.wait_ge(zeroed, 16 * 2 * U)
                sp.wait_ge(loads, 16 * 6)

            @block.gpsimd
            def _(pool):
                nc.gpsimd.memset(zeros_bf[:], 0.0).then_inc(cast, 1)
                nc.gpsimd.memset(k_stack[:], 1.0).then_inc(cast, 1)
                nc.gpsimd.memset(q_stack[:], 1.0).then_inc(cast, 1)
                nc.gpsimd.memset(values[:], 1.0)
                nc.gpsimd.memset(gates[:], 1.0)
                nc.gpsimd.memset(ones[:], 1.0)

            @block.vector
            def _(dve):
                me = Own(dve, own)
                dve.wait_ge(loads, 16 * 6)
                nc.vector.tensor_copy(ident_bf[:], ident)
                nc.vector.tensor_copy(masks_bf[:], pack[:, PACK_AT["causal_q"][0]:PACK_AT["causal_q"][0] + 6 * P])
                nc.vector.tensor_copy(same_bf[:], col("same_q"))
                nc.vector.tensor_scalar(ctx_mask_q[:].rearrange("p t k -> p (t k)"), mask_q_i, 0.0, MASKED, ALU.is_equal, ALU.mult)
                nc.vector.tensor_scalar(ctx_mask_k[:], mask_k_i, 0.0, MASKED, ALU.is_equal, ALU.mult)
                nc.vector.tensor_scalar(w_q8[:], w_q8_i, col("wscale"), None, ALU.mult)
                rest = q_tmp[0:1, 0:SE]
                me.mark(nc.vector.tensor_copy(bias_parts[:, 0, :], row("scorer")))
                me.wait()
                me.mark(nc.vector.tensor_tensor(rest, row("scorer"), bias_parts[:, 0, :], ALU.subtract))
                me.wait()
                me.mark(nc.vector.tensor_copy(bias_parts[:, 1, :], rest))
                me.wait()
                me.mark(nc.vector.tensor_tensor(bias_parts[:, 2, :], rest, bias_parts[:, 1, :], ALU.subtract))

        def inverse_root(me, y, v):
            n = v.shape[1]
            me.mark(nc.vector.tensor_scalar(y.bitcast(I32), v.bitcast(I32), -0.5, 1597463007.0, ALU.mult, ALU.add))
            me.wait()
            for _ in range(4):
                t = newton[:, 0:n]
                me.mark(nc.vector.scalar_tensor_tensor(out=t, in0=y, scalar=-0.5, in1=y, op0=ALU.mult, op1=ALU.mult))
                me.wait()
                me.mark(nc.vector.tensor_tensor(t, t, v, ALU.mult))
                me.wait()
                me.mark(nc.vector.scalar_tensor_tensor(out=y, in0=t, scalar=1.5, in1=y, op0=ALU.add, op1=ALU.mult))
                me.wait()

        def layer_norm(me, out, src, eps):
            n = src.shape[1]
            for t in range(n):
                last = nc.vector.bn_stats(stats[:, t, :], src[:, t, :])
                me.mark(last)
            me.wait()
            for t in range(n):
                me.mark(nc.vector.bn_aggr(mean_var[:, t, :], stats[:, t, :]))
            me.wait()
            me.mark(nc.vector.tensor_scalar(var_eps[:, 0:n], mean_var[:, 0:n, 1], eps, None, ALU.add))
            me.wait()
            inverse_root(me, rstd[:, 0:n], var_eps[:, 0:n])
            for t in range(n):
                me.mark(nc.vector.tensor_scalar(out[:, t, :], src[:, t, :], mean_var[:, t, 0:1], rstd[:, t:t + 1],
                                                ALU.subtract, ALU.mult))
            me.wait()

        def turn(pe, out, src, n=QT):
            for t in range(n):
                last = nc.tensor.transpose(out[:, t * P:(t + 1) * P], src[:, t, :], ident)
            return last

        def tokens_out(pe, out, lhsT, rhs, bias):
            for t in range(QT):
                last = nc.tensor.matmul(out[:, t * P:t * P + rhs.shape[-1]], lhsT[:, t * P:(t + 1) * P], rhs,
                                        start=True, stop=bias is None)
                if bias is not None:
                    last = nc.tensor.matmul(out[:, t * P:t * P + rhs.shape[-1]], ones[0:1, :], bias,
                                            start=False, stop=True)
            return last

        def attention(c):
            nk, kn, KT, name = c.nk, c.kn, c.kt, c.name
            NH = U * H

            order = []
            LAG = 8
            for t in range(NH + LAG + 7):
                if t % H == 0 and t == 0:
                    order.append(("project", 0))
                if t % H == H - 6 and t // H + 1 < U:
                    order.append(("project", t // H + 1))
                if t >= HG + 1 and (t - HG - 1) % HG == 0 and (t - HG - 1) // HG < NH // HG:
                    order.append(("rows", (t - HG - 1) // HG))
                if t < NH + LAG + 1:
                    order.append(("heads", t))
                v = t - LAG - 1 - HG
                if v >= 0 and v % HG == 0 and v // HG < NH // HG:
                    order.append(("gather", v // HG))
                for lag, task in ((2, "norm"), (3, "turn"), (4, "out"), (6, "back")):
                    v = t - LAG - lag - (H - 1)
                    if v >= 0 and v % H == 0 and v // H < U:
                        order.append((task, v // H))

            a_use, b_use = {}, {}
            for task, i in order:
                for what in {"project": ("k", "v"), "turn": ("o",), "back": ("x",)}.get(task, ()):
                    a_use[what, i] = len(a_use)
                for what in {"project": ("q",) + (("rq", "rk") if c.rope else ()), "rows": ("m",),
                             "gather": ("g",), "norm": ("l",) if c.local else (), "out": ("y",)}.get(task, ()):
                    b_use[what, i] = len(b_use)
            QD, KD = 2 * NB, 2 * NB
            K_EXTRA = (2 * 3 if c.bias is not None else 2 if c.zero_bias_rows else 0)
            kd_of = 16 * (KD + K_EXTRA)

            with Stage(nc, "max_scored", "max_taken", "exp_scored", "exp_taken", "pv_done", "a_full", "a_free",
                       "b_full", "b_free", "q_ready", "k_ready", "q_split", "k_split", "q_moved0", "q_moved1",
                       "k_moved0", "k_moved1", "rows_split", "rows_moved0", "rows_moved1", "o_copied", "normed", "out_ready", "own_dve", "own_pool") as (
                           block, max_scored, max_taken, exp_scored, exp_taken, pv_done, a_full, a_free,
                           b_full, b_free, q_ready, k_ready, q_split, k_split, q_moved0, q_moved1,
                           k_moved0, k_moved1, rows_split, rows_moved0, rows_moved1, o_copied, normed, out_ready, own_dve, own_pool):
                q_moved, k_moved = [q_moved0, q_moved1], [k_moved0, k_moved1]
                rows_moved = [rows_moved0, rows_moved1]

                @block.tensor
                def _(pe):
                    def bank_a(what, i):
                        since(pe, a_free, a_use[what, i])
                        return psA

                    def bank_b(what, i):
                        since(pe, b_free, b_use[what, i])
                        return psB

                    def scores_for_max(i, t):
                        u, h = divmod(i, H)
                        lo = 64 * (h % 2)
                        if h == 0 and t == 0:
                            pe.wait_ge(q_moved[u], 16 * QD)
                            pe.wait_ge(k_moved[u], kd_of)
                        n = QT * i + t
                        since(pe, max_taken, n - 1)
                        blocks = max_blocks(c, t)
                        out = psM[:, n % 2, :]
                        last = nc.tensor.matmul(out[:, 0:c.keys_of[t]],
                                                q_stack[lo:lo + R_MAX, u, h // 2, t * P:(t + 1) * P],
                                                k_stack[lo:lo + R_MAX, u, h // 2, 0:c.keys_of[t]],
                                                start=True, stop=not blocks)
                        for j, (at, width, m) in enumerate(blocks):
                            last = nc.tensor.matmul(out[:, at:at + width], ident_bf[:], m, start=False,
                                                    stop=j == len(blocks) - 1)
                        last.then_inc(max_scored, 1)

                    def scores_for_exp(i, k):
                        u, h = divmod(i, H)
                        lo = 64 * (h % 2)
                        if h % HG == 0 and k == 0:
                            pe.wait_ge(rows_moved[i // HG % 2], 16 * HG * (i // HG // 2 + 1))
                        n = KT * i + k
                        since(pe, exp_taken, n - 1)
                        out = psE[0:kn, n % 2, :]
                        q0 = c.first_q[k]
                        blocks = exp_blocks(c, k)
                        last = nc.tensor.matmul(out[:, q0:S], k_stack[lo:lo + R_END, u, h // 2, k * P:k * P + kn],
                                                q_stack[lo:lo + R_END, u, h // 2, q0:S], start=True,
                                                stop=not blocks)
                        for j, (at, width, m) in enumerate(blocks):
                            last = nc.tensor.matmul(out[:, at:at + width], ident_bf[0:kn, 0:kn], m,
                                                    start=False, stop=j == len(blocks) - 1)
                        last.then_inc(exp_scored, 1)

                    def times_values(i, k):
                        u, h = divmod(i, H)
                        if k == 0:
                            pe.wait_ge(exp_taken, KT * (i + 1))
                            if i % HG == 0:
                                since(pe, o_copied, i // HG - 1)
                            if h == 0:
                                pe.wait_ge(a_free, a_use["v", u] + 1)
                        lo, q0 = 32 * (i % HG), c.first_q[k]
                        last = nc.tensor.matmul(psO[lo:lo + 32, i // HG % 2, q0:S], values[0:kn, u, k, h, :],
                                                probs[0:kn, i % 2, k, q0:S], start=k == 0, stop=k == KT - 1,
                                                tile_position=(0, lo))
                        if k == KT - 1:
                            last.then_inc(pv_done, 1)

                    for task, i in order:
                        if task == "project":
                            out = bank_b("q", i)
                            nc.tensor.matmul(out[:, :], col(f"{name}_wq"), c.q(i), start=True, stop=True)\
                                .then_inc(b_full, 1)
                            out = bank_a("k", i)
                            nc.tensor.matmul(out[:, 0:nk], col(f"{name}_wk"), c.kv(i), start=True, stop=True)\
                                .then_inc(a_full, 1)
                            out = bank_a("v", i)
                            for k in range(KT):
                                has = f"{name}_bv" in ROW_AT
                                last = nc.tensor.matmul(out[0:kn, k * D:(k + 1) * D], c.kv(i)[:, k * P:k * P + kn],
                                                        col(f"{name}_wv"), start=True, stop=not has)
                                if has:
                                    last = nc.tensor.matmul(out[0:kn, k * D:(k + 1) * D], ones[0:1, 0:kn],
                                                            row(f"{name}_bv"), start=False, stop=True)
                            last.then_inc(a_full, 1)
                            if c.rope:
                                pe.wait_ge(q_ready, i + 1)
                                out = bank_b("rq", i)
                                nc.tensor.matmul(out[:, :], col("rot"), q_full, start=True, stop=True)\
                                    .then_inc(b_full, 1)
                                pe.wait_ge(k_ready, 2 * i + 1)
                                out = bank_b("rk", i)
                                nc.tensor.matmul(out[:, :], col("rot"), k_full, start=True, stop=True)\
                                    .then_inc(b_full, 1)
                        elif task == "heads":
                            for part in range(QT):
                                if i < NH:
                                    scores_for_max(i, part)
                                if 0 <= i - LAG < NH and part < KT:
                                    scores_for_exp(i - LAG, part)
                                if 0 <= i - LAG - 1 < NH and part < KT:
                                    times_values(i - LAG - 1, part)
                        elif task == "rows":
                            u, g = divmod(i, H // HG)
                            pe.wait_ge(max_taken, QT * HG * (i + 1))
                            out = bank_b("m", i)
                            for t in range(QT):
                                last = nc.tensor.transpose(out[0:HG, t * P:(t + 1) * P],
                                                           maxima[:, u, t, HG * g:HG * (g + 1)], ident)
                            last.then_inc(b_full, 1)
                        elif task == "gather":
                            pe.wait_ge(o_copied, i + 1)
                            turn(pe, bank_b("g", i), o_raw[:].rearrange("p (t n) -> p t n", n=P)).then_inc(b_full, 1)
                        elif task == "norm" and c.local:
                            out = bank_b("l", i)
                            for t in range(QT):
                                kts = [k for k, q in BAND if q == t]
                                for k in kts:
                                    at = BAND.index((k, t)) * P
                                    last = nc.tensor.matmul(out[:, t * P:(t + 1) * P], col("band", at, at + P),
                                                            values[:, i, k, :, 0:DH], start=(k == kts[0]),
                                                            stop=(k == kts[-1]))
                            last.then_inc(b_full, 1)
                        elif task == "turn":
                            pe.wait_ge(normed, i + 1)
                            turn(pe, bank_a("o", i), ot).then_inc(a_full, 1)
                        elif task == "out":
                            pe.wait_ge(a_free, a_use["o", i] + 1)
                            tokens_out(pe, bank_b("y", i), oT, col(f"{name}_wo"), row(f"{name}_bo"))\
                                .then_inc(b_full, 1)
                        elif task == "back":
                            pe.wait_ge(out_ready, i + 1)
                            turn(pe, bank_a("x", i), c.post.turned[:, i]).then_inc(a_full, 1)

                @block.scalar
                def _(act):
                    for task, i in order:
                        if task == "project":
                            act.wait_ge(a_full, a_use["k", i] + 1)
                            since(act, k_split, i)
                            bk = col(f"{name}_bk") if f"{name}_bk" in PACK_AT else 0.0
                            nc.scalar.activation(k_full[:, 0:nk], psA[:, 0:nk], ACT.Identity, bias=bk)\
                                .then_inc(a_free, 1)
                            act.wait_ge(a_free, a_use["k", i] + 1)
                            act.sem_inc(k_ready, 1)
                            act.wait_ge(a_full, a_use["v", i] + 1)
                            nc.scalar.copy(values[0:kn, i, 0:KT, :, 0:DH],
                                           psA[0:kn, 0:KT * D].rearrange("p (k h d) -> p k h d", k=KT, h=H))\
                                .then_inc(a_free, 1)
                        elif task == "heads" and 0 <= i - LAG < NH:
                            i -= LAG
                            if i >= 2:
                                act.wait_ge(pv_done, i - 1)
                            for k in range(KT):
                                n = KT * i + k
                                q0 = c.first_q[k]
                                act.wait_ge(exp_scored, n + 1)
                                nc.scalar.activation(probs[0:kn, i % 2, k, q0:S], psE[0:kn, n % 2, q0:S], ACT.Exp)\
                                    .then_inc(exp_taken, 1)
                        elif task == "gather":
                            act.wait_ge(pv_done, HG * (i + 1))
                            if i:
                                act.wait_ge(b_full, b_use["g", i - 1] + 1)
                            nc.scalar.copy(o_raw[:], psO[:, i % 2, :]).then_inc(o_copied, 1)
                        elif task == "turn":
                            act.wait_ge(a_full, a_use["o", i] + 1)
                            since(act, b_full, b_use["y", i - 1] + 1 if i else 0)
                            nc.scalar.copy(oT[:], psA[:]).then_inc(a_free, 1)
                        elif task == "back":
                            act.wait_ge(a_full, a_use["x", i] + 1)
                            if c.post.affine:
                                g, b = (col(v) for v in c.post.affine)
                                nc.scalar.activation(c.post.dest[:, i, :], psA[:], ACT.Identity, bias=b, scale=g)\
                                    .then_inc(a_free, 1)
                            else:
                                nc.scalar.copy(c.post.dest[:, i, :], psA[:]).then_inc(a_free, 1)

                @block.vector
                def _(dve):
                    me = Own(dve, own_dve)
                    for task, i in order:
                        if task == "project":
                            dve.wait_ge(b_full, b_use["q", i] + 1)
                            bq = col(f"{name}_bq") if f"{name}_bq" in PACK_AT else 0.0
                            nc.vector.tensor_scalar(q_full, psB[:], bq, c.scale, ALU.add, ALU.mult)\
                                .then_inc(b_free, 1)
                            dve.wait_ge(b_free, b_use["q", i] + 1)
                            if c.rope:
                                dve.sem_inc(q_ready, 1)
                                dve.wait_ge(b_full, b_use["rq", i] + 1)
                                nc.vector.tensor_tensor(q_tmp, psB[:], col("sin"), ALU.mult).then_inc(b_free, 1)
                                dve.wait_ge(b_free, b_use["rq", i] + 1)
                                me.mark(nc.vector.tensor_tensor(q_full, q_full, col("cos"), ALU.mult))
                                me.wait()
                                me.mark(nc.vector.tensor_tensor(q_full, q_full, q_tmp, ALU.add))
                                me.wait()
                                dve.wait_ge(b_full, b_use["rk", i] + 1)
                                nc.vector.tensor_tensor(q_tmp, psB[:], col("sin"), ALU.mult).then_inc(b_free, 1)
                                dve.wait_ge(b_free, b_use["rk", i] + 1)
                                me.mark(nc.vector.tensor_tensor(k_full, k_full, col("cos"), ALU.mult))
                                me.wait()
                                me.mark(nc.vector.tensor_tensor(k_full, k_full, q_tmp, ALU.add))
                                me.wait()
                                dve.sem_inc(k_ready, 1)
                            if i:
                                dve.wait_ge(q_moved[i - 1], 16 * QD)
                            me.mark(nc.vector.tensor_copy(q_parts[:, 0, :], q_full))
                            me.wait()
                            me.mark(nc.vector.tensor_tensor(q_tmp, q_full, q_parts[:, 0, :], ALU.subtract))
                            me.wait()
                            me.mark(nc.vector.tensor_copy(q_parts[:, 1, :], q_tmp))
                            me.wait()
                            nc.vector.tensor_tensor(q_parts[:, 2, :], q_tmp, q_parts[:, 1, :], ALU.subtract)\
                                .then_inc(q_split, 1)
                            dve.wait_ge(q_split, i + 1)
                        elif task == "heads" and i < NH:
                            u, h = divmod(i, H)
                            for t in range(QT):
                                n = QT * i + t
                                dve.wait_ge(max_scored, n + 1)
                                nc.vector.tensor_reduce(maxima[:, u, t, h:h + 1], psM[:, n % 2, 0:c.keys_of[t]],
                                                        AX_X, ALU.max).then_inc(max_taken, 1)
                        elif task == "rows":
                            dve.wait_ge(b_full, b_use["m", i] + 1)
                            since(dve, rows_moved[i % 2], 16 * HG * (i // 2))
                            me.mark(nc.vector.tensor_scalar(max_rows[:, i % 2, 0, :], psB[0:HG, :], -1.0, None,
                                                            ALU.mult))
                            me.wait()
                            nc.vector.scalar_tensor_tensor(out=max_rows[:, i % 2, 1, :], in0=psB[0:HG, :], scalar=-1.0,
                                                           in1=max_rows[:, i % 2, 0, :], op0=ALU.mult,
                                                           op1=ALU.subtract).then_inc(b_free, 1)
                            dve.wait_ge(b_free, b_use["m", i] + 1)
                            dve.sem_inc(rows_split, 1)
                        elif task == "gather":
                            u, g = divmod(i, H // HG)
                            dve.wait_ge(b_full, b_use["g", i] + 1)
                            if u and g == 0:
                                dve.wait_ge(a_free, a_use["o", u - 1] + 1)
                            sums = psB[:].rearrange("p (t h e) -> p t h e", t=QT, h=HG)
                            share = recip[:].rearrange("p (t h) -> p t h", h=HG)
                            me.mark(nc.vector.reciprocal(share, sums[:, :, :, DH]))
                            me.wait()
                            me.mark(nc.vector.tensor_tensor(
                                ot[:].rearrange("p t (h d) -> p t h d", h=H)[:, :, HG * g:HG * (g + 1), :],
                                sums[:, :, :, 0:DH], share.unsqueeze(3).to_broadcast([P, QT, HG, DH]), ALU.mult))
                            me.wait()
                            dve.sem_inc(b_free, 1)
                        elif task == "norm":
                            if c.local:
                                dve.wait_ge(b_full, b_use["l", i] + 1)
                                flat = ot[:].rearrange("p t d -> p (t d)")
                                me.mark(nc.vector.scalar_tensor_tensor(out=flat, in0=flat, scalar=0.6, in1=psB[:],
                                                                       op0=ALU.mult, op1=ALU.add))
                                me.wait()
                                dve.sem_inc(b_free, 1)
                            dve.sem_inc(normed, 1)
                        elif task == "out":
                            dve.wait_ge(b_full, b_use["y", i] + 1)
                            c.post.run(dve, me, i, psB[:].rearrange("p (t d) -> p t d", d=D), b_free)
                            dve.sem_inc(out_ready, 1)

                @block.gpsimd
                def _(pool):
                    me = Own(pool, own_pool)
                    for i in range(U):
                        pool.wait_ge(k_ready, (2 if c.rope else 1) * (i + 1))
                        if i:
                            pool.wait_ge(k_moved[i - 1], kd_of)
                        me.mark(nc.gpsimd.tensor_copy(k_parts[:, 0, 0:nk], k_full[:, 0:nk]))
                        me.wait()
                        me.mark(nc.gpsimd.tensor_tensor(k_tmp[:, 0:nk], k_full[:, 0:nk], k_parts[:, 0, 0:nk],
                                                        ALU.subtract))
                        me.wait()
                        me.mark(nc.gpsimd.tensor_copy(k_parts[:, 1, 0:nk], k_tmp[:, 0:nk]))
                        me.wait()
                        nc.gpsimd.tensor_tensor(k_parts[:, 2, 0:nk], k_tmp[:, 0:nk], k_parts[:, 1, 0:nk],
                                                ALU.subtract).then_inc(k_split, 1)

                @block.sync
                def _(sp):
                    for task, i in order:
                        if task == "project":
                            sp.wait_ge(q_split, i + 1)
                            for j, part in enumerate((0, 0, 0, 1, 1, 2)):
                                for hb in range(2):
                                    lo = 64 * hb + DH * j
                                    sp.dma_start(q_stack[lo:lo + DH, i, :, :],
                                                 q_parts[64 * hb:64 * hb + 64, part, :]).then_inc(q_moved[i], 16)
                            if c.bias is not None:
                                for hb in range(2):
                                    for r in range(3):
                                        lo = 64 * hb + R_BIAS + r
                                        sp.dma_start(k_stack[lo:lo + 1, i, :, 0:nk],
                                                     c.bias[:, r, :].unsqueeze(1).to_broadcast([1, H // 2, nk]))\
                                            .then_inc(k_moved[i], 16)
                            elif c.zero_bias_rows:
                                for hb in range(2):
                                    lo = 64 * hb + R_BIAS
                                    sp.dma_start(k_stack[lo:lo + 3, i],
                                                 zeros_bf[:].unsqueeze(1).to_broadcast([3, H // 2, S]))\
                                        .then_inc(k_moved[i], 16)
                            sp.wait_ge(k_split, i + 1)
                            for j, part in enumerate((0, 1, 2, 0, 1, 0)):
                                for hb in range(2):
                                    lo = 64 * hb + DH * j
                                    sp.dma_start(k_stack[lo:lo + DH, i, :, 0:nk],
                                                 k_parts[64 * hb:64 * hb + 64, part, 0:nk]).then_inc(k_moved[i], 16)
                        elif task == "rows":
                            u, g = divmod(i, H // HG)
                            sp.wait_ge(rows_split, i + 1)
                            for j in range(HG):
                                h = HG * g + j
                                lo = 64 * (h % 2) + R_MAX
                                sp.dma_start(q_stack[lo:lo + 2, u, h // 2, :], max_rows[j:j + 1, i % 2, :, :])\
                                    .then_inc(rows_moved[i % 2], 16)

        def max_blocks(c, t):
            if c.masks == "causal":
                return [(t * P, P, mask_at["causal_q"])]
            if c.masks == "tril2":
                return [[(0, P, mask_at["tril2_q"]), (P, P, mask_at["tril2b_q"])],
                        [(P, P, mask_at["tril2_q"])], [], []][t]
            if c.masks == "given":
                return [(0, SC, ctx_mask_q[:, t, :])]
            return []

        def exp_blocks(c, k):
            if c.masks == "causal":
                return [(k * P, P, mask_at["causal_k"])]
            if c.masks == "tril2":
                return [[(0, P, mask_at["tril2_k"])],
                        [(0, P, mask_at["tril2b_k"]), (P, P, mask_at["tril2_k"])]][k]
            if c.masks == "given":
                return [(0, S, ctx_mask_k[:])]
            return []

        def flat(ap):
            return ap.rearrange("p t d -> p (t d)")

        class Post:

            def __init__(self, run, turned, dest, affine=None):
                self.run, self.turned, self.dest, self.affine = run, turned, dest, affine

        def add_norm(dve, me, u, y, free):
            me.mark(nc.vector.tensor_tensor(flat(yt[:, u]), flat(y), flat(xt[:, u]), ALU.add))
            me.wait()
            dve.sem_inc(free, 1)
            layer_norm(me, xt[:, u], yt[:, u], 1e-5)

        def relu_add_norm(dve, me, u, y, free):
            me.mark(nc.vector.scalar_tensor_tensor(out=flat(yt[:, u]), in0=flat(y), scalar=0.0, in1=flat(xt[:, u]),
                                                   op0=ALU.max, op1=ALU.add))
            me.wait()
            dve.sem_inc(free, 1)
            layer_norm(me, yt[:, u], yt[:, u], 1e-6)

        def gain_shift(me, out, g, b):
            for t in range(QT):
                me.mark(nc.vector.tensor_tensor(out[:, t, :], out[:, t, :], col(g), ALU.mult))
            me.wait()
            for t in range(QT):
                me.mark(nc.vector.tensor_tensor(out[:, t, :], out[:, t, :], col(b), ALU.add))
            me.wait()

        def twice_norm(dve, me, u, y, free):
            me.mark(nc.vector.tensor_scalar(flat(yt[:, u]), flat(y), 0.0, 2.0, ALU.max, ALU.mult))
            me.wait()
            dve.sem_inc(free, 1)
            layer_norm(me, yt[:, u], yt[:, u], 1e-6)
            gain_shift(me, yt[:, u], "g2", "b2")

        def inner_first(dve, me, u, y, free):
            me.mark(nc.vector.tensor_tensor(flat(hres[:, u]), flat(y), flat(xt[:, u]), ALU.add))
            me.wait()
            dve.sem_inc(free, 1)
            layer_norm(me, yt[:, u], hres[:, u], 1e-5)

        def inner_second(dve, me, u, y, free):
            me.mark(nc.vector.tensor_tensor(flat(hres[:, u]), flat(y), flat(hres[:, u]), ALU.add))
            me.wait()
            dve.sem_inc(free, 1)
            layer_norm(me, yt[:, u], hres[:, u], 1e-5)

        def turn_stage(src, dest, before=None, affine=None):
            with Stage(nc, "ready", "full", "free", "own") as (block, ready, full, free, own):
                @block.vector
                def _(dve):
                    me = Own(dve, own)
                    for u in range(U):
                        if before is not None:
                            before(me, u)
                        dve.sem_inc(ready, 1)

                @block.tensor
                def _(pe):
                    for u in range(U):
                        pe.wait_ge(ready, u + 1)
                        since(pe, free, u)
                        turn(pe, psA, src[:, u]).then_inc(full, 1)

                @block.scalar
                def _(act):
                    for u in range(U):
                        act.wait_ge(full, u + 1)
                        if affine:
                            g, b = (col(v) for v in affine)
                            nc.scalar.activation(dest[:, u, :], psA[:], ACT.Identity, bias=b, scale=g).then_inc(free, 1)
                        else:
                            nc.scalar.copy(dest[:, u, :], psA[:]).then_inc(free, 1)

        def linear_stage(inT, w, bias, after, before=None):
            with Stage(nc, "ready", "a_full", "a_free", "b_full", "b_free", "done", "own") as (
                    block, ready, a_full, a_free, b_full, b_free, done, own):
                turns = 2 if before is not None else 1

                @block.vector
                def _(dve):
                    me = Own(dve, own)
                    if before is not None:
                        for u in range(U):
                            before(me, u)
                            dve.sem_inc(ready, 1)
                    for u in range(U):
                        dve.wait_ge(b_full, u + 1)
                        after(dve, me, u, psB[:].rearrange("p (t d) -> p t d", d=D), b_free)
                        dve.sem_inc(done, 1)

                @block.tensor
                def _(pe):
                    if before is not None:
                        for u in range(U):
                            pe.wait_ge(ready, u + 1)
                            since(pe, a_free, u)
                            turn(pe, psA, yt[:, u]).then_inc(a_full, 1)
                    for u in range(U):
                        if before is not None:
                            pe.wait_ge(a_free, u + 1)
                        since(pe, b_free, u)
                        tokens_out(pe, psB, inT[:, u], w, bias).then_inc(b_full, 1)
                    for u in range(U):
                        pe.wait_ge(done, u + 1)
                        since(pe, a_free, (turns - 1) * U + u)
                        turn(pe, psA, xt[:, u]).then_inc(a_full, 1)

                @block.scalar
                def _(act):
                    for n in range(turns * U):
                        act.wait_ge(a_full, n + 1)
                        dest = xT if n >= (turns - 1) * U else inT
                        nc.scalar.copy(dest[:, n % U, :], psA[:]).then_inc(a_free, 1)

        def l0x_tail(dve, me, u, y, free):
            me.mark(nc.vector.scalar_tensor_tensor(out=flat(yt[:, u]), in0=flat(y), scalar=0.0, in1=flat(yt[:, u]),
                                                   op0=ALU.max, op1=ALU.add))
            me.wait()
            dve.sem_inc(free, 1)
            layer_norm(me, yt[:, u], yt[:, u], 1e-6)
            gain_shift(me, yt[:, u], "g3", "b3")
            me.mark(nc.vector.tensor_tensor(flat(yt[:, u]), flat(yt[:, u]), flat(xt[:, u]), ALU.add))
            me.wait()
            layer_norm(me, xt[:, u], yt[:, u], 1e-5)

        def quantize(me, u):
            sq, q = ot, probs[:, 0, 0:1, :].rearrange("p a (t d) -> p (a t) d", d=D)
            a, b = rstd[:], r1[:]
            me.mark(nc.vector.tensor_tensor(flat(sq[:]), flat(xt[:, u]), flat(xt[:, u]), ALU.mult))
            me.wait()
            me.mark(nc.vector.tensor_reduce(a, sq[:], AX_X, ALU.add))
            me.wait()
            me.mark(nc.vector.tensor_scalar(var_eps[:], a, 1.0 / D, 1e-6, ALU.mult, ALU.add))
            me.wait()
            inverse_root(me, a, var_eps[:])
            for t in range(QT):
                me.mark(nc.vector.tensor_scalar(yt[:, u, t, :], xt[:, u, t, :], rstd[:, t:t + 1], None, ALU.mult))
            me.wait()
            me.mark(nc.vector.scalar_tensor_tensor(out=flat(sq[:]), in0=flat(yt[:, u]), scalar=-1.0, in1=flat(yt[:, u]),
                                                   op0=ALU.mult, op1=ALU.max))
            me.wait()
            me.mark(nc.vector.tensor_reduce(b, sq[:], AX_X, ALU.max))
            me.wait()
            me.mark(nc.vector.tensor_scalar(b, b, 1e-5, None, ALU.max))
            me.wait()
            me.mark(nc.vector.reciprocal(b, b))
            me.wait()
            me.mark(nc.vector.tensor_scalar(b, b, 127.0, None, ALU.mult))
            me.wait()
            for t in range(QT):
                me.mark(nc.vector.tensor_scalar(q[:, t, :], yt[:, u, t, :], r1[:, t:t + 1], None, ALU.mult))
            me.wait()
            me.mark(nc.vector.tensor_scalar(flat(q), flat(q), 12582912.0, None, ALU.add))
            me.wait()
            me.mark(nc.vector.tensor_scalar(flat(q), flat(q), -12582912.0, 127.0, ALU.add, ALU.min))
            me.wait()
            me.mark(nc.vector.tensor_scalar(flat(q), flat(q), -128.0, None, ALU.max))
            me.mark(nc.vector.reciprocal(a, b))
            me.wait()
            for t in range(QT):
                me.mark(nc.vector.scalar_tensor_tensor(out=q[:, t, :], in0=q[:, t, :], scalar=rstd[:, t:t + 1],
                                                       in1=yt[:, u, t, :], op0=ALU.mult, op1=ALU.subtract))
            me.wait()
            me.mark(nc.vector.tensor_tensor(flat(yt[:, u]), flat(yt[:, u]), flat(q), ALU.add))
            me.wait()

        def mlp_stage():
            with Stage(nc, "h_full", "h_done", "y_full", "y_free", "x_done", "a_full", "own") as (
                    block, h_full, h_done, y_full, y_free, x_done, a_full, own):
                @block.tensor
                def _(pe):
                    for u in range(U):
                        for f in range(FT1):
                            n = FT1 * u + f
                            since(pe, h_done, n - 1)
                            nc.tensor.matmul(psE[:, n % 2, :], col("fc", f * P, (f + 1) * P), nT[:, u, :], start=True,
                                             stop=True).then_inc(h_full, 1)
                        pe.wait_ge(h_done, FT1 * (u + 1))
                        since(pe, y_free, u)
                        for t in range(QT):
                            for f in range(FT1):
                                nc.tensor.matmul(psB[:, t * P:(t + 1) * P], probs[:, u % 2, f, t * P:(t + 1) * P],
                                                 col("mlp", f * D, (f + 1) * D), start=f == 0, stop=False)
                            last = nc.tensor.matmul(psB[:, t * P:(t + 1) * P], ones[0:1, :], row("mlp_b"),
                                                    start=False, stop=True)
                        last.then_inc(y_full, 1)
                    for u in range(U):
                        pe.wait_ge(x_done, 2 * u + 1)
                        turn(pe, psA, xt[:, u]).then_inc(a_full, 1)
                        pe.wait_ge(x_done, 2 * u + 2)

                @block.scalar
                def _(act):
                    for n in range(U * FT1):
                        u, f = divmod(n, FT1)
                        act.wait_ge(h_full, n + 1)
                        nc.scalar.activation(probs[:, u % 2, f, :], psE[:, n % 2, :], ACT.Gelu_apprx_tanh,
                                             bias=col("fc_b", f, f + 1)).then_inc(h_done, 1)
                    for u in range(U):
                        act.wait_ge(a_full, u + 1)
                        nc.scalar.copy(xT[:, u, :], psA[:]).then_inc(x_done, 1)

                @block.vector
                def _(dve):
                    me = Own(dve, own)
                    for u in range(U):
                        dve.wait_ge(y_full, u + 1)
                        me.mark(nc.vector.tensor_tensor(flat(hres[:, u]), psB[:], flat(hres[:, u]), ALU.add))
                        me.wait()
                        dve.sem_inc(y_free, 1)
                        me.mark(nc.vector.tensor_tensor(flat(yt[:, u]), flat(hres[:, u]), flat(xt[:, u]), ALU.add))
                        me.wait()
                        layer_norm(me, xt[:, u], yt[:, u], 1e-5)
                        if u:
                            dve.wait_ge(x_done, 2 * u)
                        dve.sem_inc(x_done, 1)

        def route(me, u, n_exp, top, bank):
            lg, pr, pk = logits[:, :, 0:n_exp], rprobs[:, :, 0:n_exp], pick[:, :, 0:n_exp]
            gt = gates[:, u, :, 0:n_exp]
            wide = [P, QT, n_exp]

            def per_token(ap):
                return ap.unsqueeze(2).to_broadcast(wide)

            src = bank[:].rearrange("p (t e) -> p t e", t=QT)[:, :, 0:n_exp]
            iota = col("iota", 0, n_exp).unsqueeze(1).to_broadcast(wide)
            me.mark(nc.vector.tensor_reduce(r1[:], src, AX_X, ALU.max))
            me.wait()
            me.mark(nc.vector.tensor_tensor(lg, src, per_token(r1[:]), ALU.subtract))
            me.wait()
            return lg, pr, pk, gt, per_token, iota

        def choose(me, top, lg, pr, pk, gt, per_token, iota):
            me.mark(nc.vector.tensor_reduce(r1[:], lg, AX_X, ALU.add))
            me.wait()
            me.mark(nc.vector.reciprocal(rstd[:], r1[:]))
            me.wait()
            me.mark(nc.vector.tensor_tensor(pr, lg, per_token(rstd[:]), ALU.mult))
            me.wait()
            for k in range(top):
                me.mark(nc.vector.tensor_reduce(r1[:], pr, AX_X, ALU.max))
                me.wait()
                me.mark(nc.vector.tensor_tensor(pk, pr, per_token(r1[:]), ALU.not_equal))
                me.wait()
                me.mark(nc.vector.scalar_tensor_tensor(out=pk, in0=pk, scalar=64.0, in1=iota, op0=ALU.mult, op1=ALU.add))
                me.wait()
                me.mark(nc.vector.tensor_reduce(rstd[:], pk, AX_X, ALU.min))
                me.wait()
                me.mark(nc.vector.tensor_tensor(pk, iota, per_token(rstd[:]), ALU.is_equal))
                me.wait()
                if k == 0:
                    me.mark(nc.vector.tensor_tensor(gt, pk, per_token(r1[:]), ALU.mult))
                else:
                    me.mark(nc.vector.tensor_tensor(lg, pk, per_token(r1[:]), ALU.mult))
                    me.wait()
                    me.mark(nc.vector.tensor_tensor(gt, gt, lg, ALU.add))
                if k < top - 1:
                    me.mark(nc.vector.scalar_tensor_tensor(out=pr, in0=pk, scalar=-4.0, in1=pr, op0=ALU.mult,
                                                           op1=ALU.add))
                me.wait()

        def moe_stage(li, n_exp, n_routed, top, ft, func, weights, per_slot, store=None,
                      residuals=1):
            b1 = f"e{li}_b1"
            J = U * n_exp
            RING = 4
            only_act = func != ACT.Relu

            def hidden_bank(n):
                if only_act:
                    return psM[:, n % 2, :]
                return (psM if n % 2 == 0 else psE)[:, n // 2 % 2, :]

            with Stage(nc, "w_loaded0", "w_loaded1", "w_loaded2", "w_loaded3", "r_full", "r_max", "r_exp", "g_ready", "b_full", "b_free", "a_full", "a_free",
                       "h_full", "act_h", "dve_h", "down", "taken", "x_done", "own", "stored") as (
                           block, w_loaded0, w_loaded1, w_loaded2, w_loaded3, r_full, r_max, r_exp, g_ready, b_full, b_free, a_full, a_free,
                           h_full, act_h, dve_h, down, taken, x_done, own, stored):

                w_loaded = [w_loaded0, w_loaded1, w_loaded2, w_loaded3]

                def hidden_taken(eng, n):
                    if only_act:
                        since(eng, act_h, n)
                    else:
                        since(eng, act_h, (n + 1) // 2)
                        since(eng, dve_h, n // 2)

                @block.sync
                def _(sp):
                    for n in range(J // per_slot):
                        since(sp, down, per_slot * (n - RING + 1))
                        sp.dma_start(experts[:, n % RING, :], io[weights][n % (n_exp // per_slot)])\
                            .then_inc(w_loaded[n % RING], 16)
                    if store is not None:
                        for u in range(U):
                            sp.wait_ge(x_done, u + 1)
                            sp.dma_start(store(u), xt[:, u:u + 1]).then_inc(stored, 16)
                        sp.wait_ge(stored, 16 * U)

                def w_of(j, up, f):
                    at = (j % per_slot) * 2 * ft * P + (0 if up else ft * P) + f * P
                    return experts[:, j // per_slot % RING, at:at + P]

                @block.tensor
                def _(pe):
                    def up(j):
                        u = j // n_exp
                        n = j // per_slot
                        pe.wait_ge(w_loaded[n % RING], 16 * (n // RING + 1))
                        for f in range(ft):
                            n = ft * j + f
                            if only_act:
                                since(pe, act_h, n - 1)
                            elif n % 2 == 0:
                                since(pe, act_h, n // 2 - 1)
                            else:
                                since(pe, dve_h, n // 2 - 1)
                            nc.tensor.matmul(hidden_bank(n), w_of(j, True, f), xT[:, u, :], start=True, stop=True)\
                                .then_inc(h_full, 1)

                    def down_proj(j):
                        hidden_taken(pe, ft * (j + 1))
                        since(pe, taken, j - 1)
                        for t in range(QT):
                            for f in range(ft):
                                last = nc.tensor.matmul(psO[:, j % 2, t * P:(t + 1) * P],
                                                        probs[:, j % 2, f, t * P:(t + 1) * P], w_of(j, False, f),
                                                        start=f == 0, stop=f == ft - 1)
                        last.then_inc(down, 1)

                    for u in range(U):
                        since(pe, b_free, 2 * u)
                        tokens_out(pe, psB, xT[:, u], col(f"wr{li}"), row(f"br{li}")).then_inc(b_full, 1)
                        up(u * n_exp)
                        pe.wait_ge(g_ready, u + 1)
                        since(pe, a_free, u)
                        for t in range(QT):
                            last = nc.tensor.transpose(psA[0:n_exp, t * P:(t + 1) * P], gates[:, u, t, 0:n_exp], ident)
                        last.then_inc(a_full, 1)
                        for e in range(n_exp):
                            j = u * n_exp + e
                            if e + 1 < n_exp:
                                up(j + 1)
                            if e == 0:
                                pe.wait_ge(a_free, u + 1)
                                pe.wait_ge(b_free, 2 * u + 1)
                                for t in range(QT):
                                    last = nc.tensor.matmul(psB[:, t * P:(t + 1) * P],
                                                            gatesT[0:n_exp, u, t * P:(t + 1) * P],
                                                            e_b2[0:n_exp, li - 1, :], start=True, stop=True)
                                last.then_inc(b_full, 1)
                            down_proj(j)
                    if store is None:
                        for u in range(U):
                            pe.wait_ge(x_done, u + 1)
                            since(pe, a_free, U + u)
                            turn(pe, psA, xt[:, u]).then_inc(a_full, 1)

                def hidden(eng, j, f):
                    u, n = j // n_exp, ft * j + f
                    e = j % n_exp
                    eng.wait_ge(h_full, n + 1)
                    if f < 2:
                        since(eng, down, j - 1)
                    return probs[:, j % 2, f, :], hidden_bank(n), col(b1, e * ft + f, e * ft + f + 1)

                @block.scalar
                def _(act):
                    for u in range(U):
                        act.wait_ge(r_max, u + 1)
                        nc.scalar.activation(logits[:, :, 0:n_routed], logits[:, :, 0:n_routed], ACT.Exp)\
                            .then_inc(r_exp, 1)
                        for e in range(n_exp):
                            j = u * n_exp + e
                            for f in range(ft):
                                if only_act or (ft * j + f) % 2 == 0:
                                    out, src, bias = hidden(act, j, f)
                                    nc.scalar.activation(out, src, func, bias=bias).then_inc(act_h, 1)
                            if e == 0:
                                act.wait_ge(a_full, u + 1)
                                nc.scalar.copy(gatesT[0:n_exp, u, :], psA[0:n_exp, :]).then_inc(a_free, 1)
                    if store is None:
                        for u in range(U):
                            act.wait_ge(a_full, U + u + 1)
                            nc.scalar.copy(xT[:, u, :], psA[:]).then_inc(a_free, 1)

                def gated(dve, me, j):
                    u, e = divmod(j, n_exp)
                    dve.wait_ge(down, j + 1)
                    me.wait()
                    for t in range(QT):
                        last = nc.vector.scalar_tensor_tensor(out=hres[:, u, t, :], in0=psO[:, j % 2, t * P:(t + 1) * P],
                                                              scalar=gates[:, u, t, e:e + 1], in1=hres[:, u, t, :],
                                                              op0=ALU.mult, op1=ALU.add)
                        me.mark(last)
                    me.wait()
                    dve.sem_inc(taken, 1)

                @block.vector
                def _(dve):
                    me = Own(dve, own)

                    def hidden_of(j):
                        for f in range(ft):
                            if not only_act and (ft * j + f) % 2 == 1:
                                out, src, bias = hidden(dve, j, f)
                                nc.vector.tensor_scalar(out, src, bias, 0.0, ALU.add, ALU.max).then_inc(dve_h, 1)

                    for u in range(U):
                        dve.wait_ge(b_full, 2 * u + 1)
                        state = route(me, u, n_routed, top, psB)
                        dve.sem_inc(b_free, 1)
                        dve.sem_inc(r_max, 1)
                        dve.wait_ge(r_exp, u + 1)
                        choose(me, top, *state)
                        dve.sem_inc(g_ready, 1)
                        for e in range(n_exp):
                            j = u * n_exp + e
                            hidden_of(j)
                            if e == 0:
                                dve.wait_ge(b_full, 2 * u + 2)
                                me.mark(nc.vector.scalar_tensor_tensor(out=flat(hres[:, u]), in0=flat(xt[:, u]),
                                                                       scalar=float(residuals), in1=psB[:],
                                                                       op0=ALU.mult, op1=ALU.add))
                                me.wait()
                                dve.sem_inc(b_free, 1)
                            if e > 0:
                                gated(dve, me, j - 1)
                        gated(dve, me, (u + 1) * n_exp - 1)
                        me.wait()
                        layer_norm(me, xt[:, u], hres[:, u], 1e-5)
                        dve.sem_inc(x_done, 1)

        def group_attention(first):
            HB = 4
            NG = LH // HB
            xg = nT[:].rearrange("p u s -> p (u s)").rearrange("p (g n) -> p g n", n=P)
            xg_t = yt[:].rearrange("p u t d -> p (u t) d")
            new_t = hres[:].rearrange("p u t d -> p (u t) d")
            qT3 = probs[:, 0].rearrange("p a s -> p (a s)")[:, 0:LP].rearrange("p (j n) -> p j n", n=P)
            kT3 = probs[:, 0].rearrange("p a s -> p (a s)")[:, LP:2 * LP].rearrange("p (j n) -> p j n", n=P)
            v3 = values[:].rearrange("p u t h e -> p (u t h e)")[:, 0:LH * (LD + 1)].rearrange(
                "p (h e) -> p h e", e=LD + 1)
            p3 = probs[:, 1, 0:2, :]
            pT3 = probs[:, 1, 2:4, :]
            o3 = work[:, 0:2].rearrange("p a s -> p (a s)")
            oT3 = work[:, 2:4].rearrange("p a s -> p (a s)")
            mx3, rc3 = maxima[:, 0], recip
            heads_of = [[8 * (g // 2) + g % 2 + 2 * j for j in range(HB)] for g in range(NG)]

            with Stage(nc, "x_in", "x_out", "b_full", "b_free", "a_full", "a_free", "s_full", "s_free", "p_ready",
                       "t_full", "t_free", "pv_full", "pv_free", "o_done", "x_done", "own", "shifted") as (
                           block, x_in, x_out, b_full, b_free, a_full, a_free, s_full, s_free, p_ready,
                           t_full, t_free, pv_full, pv_free, o_done, x_done, own, shifted):
                @block.sync
                def _(sp):
                    for w in range(U3):
                        sp.dma_start(xg[:, w, :].rearrange("p (b n) -> p b n", b=B),
                                     x_all[:, :, bass.ds(first + w * G3, G3)]).then_inc(x_in, 16)
                    for w in range(U3):
                        sp.wait_ge(a_free, 4 * (w + 1))
                        sp.dma_start(x_all[:, :, bass.ds(first + w * G3, G3)],
                                     xg[:, w, :].rearrange("p (b n) -> p b n", b=B)).then_inc(x_out, 16)
                    sp.wait_ge(x_out, 16 * U3)

                @block.tensor
                def _(pe):
                    for w in range(U3):
                        pe.wait_ge(x_in, 16 * U3)
                        x_w = xg[:, w, :]
                        since(pe, a_free, 4 * w)
                        nc.tensor.transpose(psA[:, 0:P], x_w, ident).then_inc(a_full, 1)
                        for n in range(4):
                            since(pe, b_free, 7 * w + n)
                            if n == 0 and w:
                                pe.wait_ge(pv_full, NG * w)
                            for j in range(4):
                                at = (n // 2) * LP + ((n % 2) * 4 + j) * P
                                last = nc.tensor.matmul(psB[:, j * P:(j + 1) * P], in_w[:, at:at + P], x_w,
                                                        start=True, stop=True)
                            last.then_inc(b_full, 1)
                        for n in range(2):
                            since(pe, b_free, 7 * w + 4 + n)
                            nc.tensor.matmul(psB[:, :], x_w, in_w[:, 2 * LP + n * 512:2 * LP + (n + 1) * 512],
                                             start=True, stop=True).then_inc(b_full, 1)

                        def scores(g):
                            m = NG * w + g
                            pe.wait_ge(b_free, 7 * w + 4)
                            since(pe, s_free, m - 1)
                            out = psM[:, m % 2, :]
                            nc.tensor.matmul(out, ident_bf[:], same_bf[:], start=True, stop=False)
                            for j, h in enumerate(heads_of[g]):
                                lo = LD * (h % 2)
                                last = nc.tensor.matmul(out[:, j * P:(j + 1) * P], qT3[lo:lo + LD, h // 2, :],
                                                        kT3[lo:lo + LD, h // 2, :], start=False, stop=j == HB - 1)
                            last.then_inc(s_full, 1)

                        def turned(g):
                            m = NG * w + g
                            pe.wait_ge(p_ready, m + 1)
                            since(pe, t_free, m - 1)
                            for j in range(HB):
                                last = nc.tensor.transpose(psE[:, m % 2, j * P:(j + 1) * P],
                                                           p3[:, m % 2, j * P:(j + 1) * P], ident)
                            last.then_inc(t_full, 1)

                        def pv(g):
                            m = NG * w + g
                            pe.wait_ge(t_free, m + 1)
                            pe.wait_ge(b_free, 7 * w + 6)
                            since(pe, pv_free, m - 1)
                            for j, h in enumerate(heads_of[g]):
                                last = nc.tensor.matmul(psO[:, m % 2, j * (LD + 1):(j + 1) * (LD + 1)],
                                                        pT3[:, m % 2, j * P:(j + 1) * P], v3[:, h, :],
                                                        start=True, stop=True)
                            last.then_inc(pv_full, 1)

                        for g in range(NG + 2):
                            if g < NG:
                                scores(g)
                            if 1 <= g <= NG:
                                turned(g - 1)
                            if g >= 2:
                                pv(g - 2)
                        pe.wait_ge(pv_free, NG * (w + 1))
                        for n in range(2):
                            pe.wait_ge(a_free, 4 * w + 1 + n)
                            turn(pe, psA, o3[:, n * 512:(n + 1) * 512].rearrange("p (t d) -> p t d", d=P))\
                                .then_inc(a_full, 1)
                        pe.wait_ge(a_free, 4 * w + 3)
                        for j in range(LP // P):
                            nc.tensor.matmul(psB[:, 0:D], oT3[:, j * P:(j + 1) * P], out_w[:, j, :], start=j == 0,
                                             stop=False)
                        nc.tensor.matmul(psB[:, 0:D], ones[0:1, :], row("l3_bo"), start=False, stop=True)\
                            .then_inc(b_full, 1)
                        pe.wait_ge(x_done, w + 1)
                        nc.tensor.transpose(psA[:, 0:P], new_t[:, w, :], ident).then_inc(a_full, 1)

                @block.scalar
                def _(act):
                    for w in range(U3):
                        act.wait_ge(a_full, 4 * w + 1)
                        nc.scalar.copy(xg_t[:, w, :], psA[:, 0:P]).then_inc(a_free, 1)

                        def exp(g):
                            m = NG * w + g
                            act.wait_ge(shifted, m + 1)
                            nc.scalar.activation(p3[:, m % 2, :], p3[:, m % 2, :], ACT.Exp, scale=LD ** -0.5)\
                                .then_inc(p_ready, 1)

                        def keys_first(g):
                            m = NG * w + g
                            act.wait_ge(t_full, m + 1)
                            since(act, pv_full, m - 1)
                            nc.scalar.copy(pT3[:, m % 2, :], psE[:, m % 2, :]).then_inc(t_free, 1)

                        for g in range(NG + 1):
                            if g < NG:
                                exp(g)
                            if g >= 1:
                                keys_first(g - 1)
                        for n in range(2):
                            act.wait_ge(a_full, 4 * w + 2 + n)
                            if n == 0:
                                since(act, b_full, 7 * w)
                            nc.scalar.copy(oT3[:, n * 512:(n + 1) * 512], psA[:]).then_inc(a_free, 1)
                        act.wait_ge(a_full, 4 * w + 4)
                        nc.scalar.copy(xg[:, w, :], psA[:, 0:P]).then_inc(a_free, 1)

                @block.vector
                def _(dve):
                    me = Own(dve, own)
                    me.mark(nc.vector.memset(v3[:, :, LD:LD + 1], 1.0))
                    for w in range(U3):
                        for n in range(4):
                            dve.wait_ge(b_full, 7 * w + n + 1)
                            if n == 0:
                                since(dve, s_full, NG * w)
                            dest = (qT3 if n < 2 else kT3)[:, (n % 2) * 4:(n % 2) * 4 + 4, :]
                            bias = col("l3_bq" if n < 2 else "l3_bk", (n % 2) * 4, (n % 2) * 4 + 4)
                            nc.vector.tensor_tensor(dest, psB[:].rearrange("p (j n) -> p j n", n=P),
                                                    bias.unsqueeze(2).to_broadcast([P, 4, P]), ALU.add)\
                                .then_inc(b_free, 1)
                        for n in range(2):
                            dve.wait_ge(b_full, 7 * w + 5 + n)
                            nc.vector.tensor_tensor(v3[:, 8 * n:8 * n + 8, 0:LD],
                                                    psB[:].rearrange("p (h d) -> p h d", d=LD),
                                                    l3_bv[n].rearrange("p (h d) -> p h d", d=LD),
                                                    ALU.add).then_inc(b_free, 1)

                        def shift(g):
                            m = NG * w + g
                            dve.wait_ge(s_full, m + 1)
                            since(dve, t_full, m - 1)
                            s3 = psM[:, m % 2, :].rearrange("p (j n) -> p j n", n=P)
                            top = mx3[:, g, 0:HB]
                            me.mark(nc.vector.tensor_reduce(top, s3, AX_X, ALU.max))
                            me.wait()
                            nc.vector.tensor_tensor(p3[:, m % 2, :].rearrange("p (j n) -> p j n", n=P), s3,
                                                    top.unsqueeze(2).to_broadcast([P, HB, P]), ALU.subtract)\
                                .then_inc(s_free, 1)
                            dve.wait_ge(s_free, m + 1)
                            dve.sem_inc(shifted, 1)

                        def normalise(g):
                            m = NG * w + g
                            dve.wait_ge(pv_full, m + 1)
                            if g == 0:
                                since(dve, a_full, 4 * (w - 1) + 3 if w else 0)
                            out = psO[:, m % 2, 0:HB * (LD + 1)].rearrange("p (j e) -> p j e", e=LD + 1)
                            rc = rc3[:, 4 * g:4 * g + 4]
                            me.mark(nc.vector.reciprocal(rc, out[:, :, LD]))
                            me.wait()
                            first_h = heads_of[g][0]
                            dest = o3.rearrange("p (h d) -> p h d", d=LD)[:, first_h:first_h + 2 * HB - 1:2, :]
                            nc.vector.tensor_tensor(dest, out[:, :, 0:LD],
                                                    rc.unsqueeze(2).to_broadcast([P, HB, LD]), ALU.mult)\
                                .then_inc(pv_free, 1)

                        for g in range(NG + 2):
                            if g < NG:
                                shift(g)
                            if g >= 2:
                                normalise(g - 2)
                        dve.wait_ge(b_full, 7 * w + 7)
                        dve.wait_ge(a_free, 4 * w + 1)
                        me.mark(nc.vector.tensor_tensor(new_t[:, w, :], psB[:, 0:D], xg_t[:, w, :], ALU.add))
                        me.wait()
                        dve.sem_inc(b_free, 1)
                        layer_norm(me, new_t[:, w:w + 1, :], new_t[:, w:w + 1, :], 1e-5)
                        dve.sem_inc(x_done, 1)

        l3_bv = [flat(hres[:, 1]), flat(yt[:, 1])]

        def load_units(pair):
            with Stage(nc, "in_x") as (block, in_x):
                @block.sync
                def _(sp):
                    for u in range(U):
                        b = bass.ds(pair * U + u, 1)
                        sp.dma_start(xt[:, u:u + 1], io["x"].rearrange("b (t p) d -> p b t d", p=P)[:, b])\
                            .then_inc(in_x, 16)
                        sp.dma_start(ctxT[:, u:u + 1, :], io["ctxT"][:, b, :]).then_inc(in_x, 16)
                    sp.wait_ge(in_x, 32 * U)

        x_unit = lambda u: xT[:, u, :]
        n_unit = lambda u: nT[:, u, :]
        ctx_unit = lambda u: ctxT[:, u, :]
        enc_unit = lambda u: col("enc")
        std = Post(add_norm, xt, xT)

        with nc.Fori(0, B // U) as pair:
            load_units(pair)
            turn_stage(xt, xT)
            attention(Attention("L0a", x_unit, x_unit, S, DH ** -0.5, std, rope=True))
            attention(Attention("L0s", x_unit, x_unit, S, S ** -0.5, Post(relu_add_norm, yt, nT, ("g1", "b1")),
                                masks="causal"))
            attention(Attention("L0c", n_unit, ctx_unit, SC, SC ** -0.5, Post(twice_norm, yt, nT)))
            linear_stage(nT, col("wf"), row("bf"), l0x_tail)
            linear_stage(nT, w_q8[:], row("q8_b"), add_norm, before=quantize)
            attention(Attention("L1a", x_unit, x_unit, S, DH ** -0.5, std, local=True))
            attention(Attention("L1c", x_unit, ctx_unit, SC, DH ** -0.5, std, masks="given"))
            moe_stage(1, E1, E1, K1, FT1, ACT.Relu, "experts1", 1)
            turn_stage(yt, nT, before=lambda me, u: layer_norm(me, yt[:, u], xt[:, u], 1e-5), affine=("ln1_g", "ln1_b"))
            attention(Attention("L2s", n_unit, n_unit, S, DH ** -0.5, Post(inner_first, yt, nT, ("lnx_g", "lnx_b")),
                                masks="causal"))
            attention(Attention("L2c", n_unit, enc_unit, SE, DH ** -0.5,
                                Post(inner_second, yt, nT, ("ln2_g", "ln2_b")), masks="tril2", bias=bias_parts[:]))
            mlp_stage()
            attention(Attention("L2x", x_unit, ctx_unit, SC, DH ** -0.5, std, zero_bias_rows=True))
            moe_stage(2, E2, E2, K2, FT1, ACT.Relu, "experts2", 1)
            with Stage(nc, "kept") as (block, kept):
                @block.sync
                def _(sp):
                    for u in range(U):
                        sp.dma_start(x_all[:, bass.ds(pair * U + u, 1), :], xT[:, u:u + 1, :]).then_inc(kept, 16)
                    sp.wait_ge(kept, 16 * U)

        with Stage(nc, "dummy") as (block, dummy):
            @block.sync
            def _(sp):
                sp.dma_start(in_w, io["in_w"]).then_inc(loads3, 16)
                sp.dma_start(out_w, io["out_w"]).then_inc(loads3, 16)
                for n in range(2):
                    sp.dma_start(l3_bv[n], io["l3_bv"][:, n * 512:(n + 1) * 512]).then_inc(loads3, 16)
                sp.wait_ge(loads3, 16 * 4)

        with nc.Fori(0, S // G3 // U3) as chunk:
            group_attention(chunk * (U3 * G3))

        with Stage(nc, "dummy2") as (block, dummy2):
            @block.gpsimd
            def _(pool):
                nc.gpsimd.memset(values[:], 1.0)

        with nc.Fori(0, B // U) as pair:
            with Stage(nc, "in_x", "full", "free") as (block, in_x, full, free):
                @block.sync
                def _(sp):
                    for u in range(U):
                        b = bass.ds(pair * U + u, 1)
                        sp.dma_start(xT[:, u:u + 1, :], x_all[:, b, :]).then_inc(in_x, 16)
                        sp.dma_start(ctxT[:, u:u + 1, :], io["ctxT"][:, b, :]).then_inc(in_x, 16)
                    sp.wait_ge(in_x, 32 * U)

                @block.tensor
                def _(pe):
                    pe.wait_ge(in_x, 32 * U)
                    for u in range(U):
                        since(pe, free, u)
                        turn(pe, psA, xT[:, u].rearrange("p (t n) -> p t n", n=P)).then_inc(full, 1)

                @block.scalar
                def _(act):
                    for u in range(U):
                        act.wait_ge(full, u + 1)
                        nc.scalar.copy(flat(xt[:, u]), psA[:]).then_inc(free, 1)

            attention(Attention("L3c", x_unit, ctx_unit, SC, DH ** -0.5, std))
            moe_stage(3, E3, E3 - 1, K3, 1, ACT.Gelu, "experts3", 4, residuals=2,
                      store=lambda u: io["out"].rearrange("b (t p) d -> p b t d", p=P)[:, bass.ds(pair * U + u, 1)])


def kernel(**a):
    import concourse.bacc as bacc
    from concourse.bass_utils import run_bass_kernel_spmd

    a = {k: np.asarray(v) for k, v in a.items()}
    perm = np.array([(2 * pr + hb) * DH + d for hb in range(2) for d in range(DH) for pr in range(H // 2)])

    t = {}
    f = np.float32
    t["ident"] = np.eye(P, dtype=f)
    d_of = np.array([d for _ in range(2) for d in range(DH) for _ in range(H // 2)])
    rot = np.zeros((P, P), f)
    for m in range(P):
        hb, d, pr = m // 64, m // 8 % 8, m % 8
        other = hb * 64 + (d ^ 1) * 8 + pr
        rot[other, m] = -1.0 if d % 2 == 0 else 1.0
    t["rot"] = rot
    freqs = np.arange(DH // 2, dtype=f) * f(1.0 / 10000.0)
    angles = np.arange(S, dtype=f)[:, None] * freqs[None, :]
    t["cos"] = np.cos(angles).astype(f)[:, d_of // 2].T
    t["sin"] = np.sin(angles).astype(f)[:, d_of // 2].T
    i = np.arange(P)
    later = np.where(i[None, :] > i[:, None], MASKED, 0.0)
    later2 = np.where(i[None, :] > i[:, None] + 2, MASKED, 0.0)
    later2b = np.where(i[None, :] + P > i[:, None] + 2, MASKED, 0.0)
    for n, m in (("causal", later), ("tril2", later2), ("tril2b", later2b)):
        t[f"{n}_q"], t[f"{n}_k"] = m, m.T
    same = np.where(i[None, :] % G3 == i[:, None] % G3, 0.0, MASKED)
    t["same_q"] = np.tile(same, (1, 4))
    j = np.arange(S)
    dist = j[:, None] - j[None, :]
    local = np.where(np.abs(dist) <= 3, np.exp(-dist.astype(f) ** 2 / f(2.0 * 0.4 ** 2)), 0.0).astype(f)
    local = (1.0 - 0.6) * (local / (local.sum(-1, keepdims=True) + 1e-10))
    t["band"] = np.concatenate([local[q * P:(q + 1) * P, k * P:(k + 1) * P].T for k, q in BAND], 1)
    t["iota"] = np.tile(np.arange(32), (P, 1))

    def heads(w):
        return w.transpose(1, 0, 2).reshape(D, D)

    c = a["L2_attn_c_attn_w"]
    kv = a["L2_attn_x_kv_w"]
    cb, kb = a["L2_attn_c_attn_b"], a["L2_attn_x_kv_b"]
    att = {
        "L0a": [a[f"L0_attn_W{n}"].T for n in "qkvo"] + [a[f"L0_attn_b{n}"] for n in "qkvo"],
        "L0s": [heads(a[f"L0_xattn_W{n}1"]) for n in "qkv"] + [a["L0_xattn_Wo1"], None, None, None, a["L0_xattn_bo1"]],
        "L0c": [heads(a[f"L0_xattn_W{n}2"]) for n in "qkv"] + [a["L0_xattn_Wo2"], None, None, None, a["L0_xattn_bo2"]],
        "L1a": [a[f"L1_attn_W{n}"].T for n in "qkvo"] + [a[f"L1_attn_b{n}"] for n in "qkvo"],
        "L1c": [a[f"L1_xattn_W{n}"].T for n in "qkvo"] + [a[f"L1_xattn_b{n}"] for n in "qkvo"],
        "L2s": [c[:, 0:D], c[:, D:2 * D], c[:, 2 * D:], a["L2_attn_attn_proj_w"], cb[0:D], cb[D:2 * D], cb[2 * D:],
                a["L2_attn_attn_proj_b"]],
        "L2c": [a["L2_attn_q_attn_w"], kv[:, 0:D], kv[:, D:], a["L2_attn_x_proj_w"], a["L2_attn_q_attn_b"], kb[0:D],
                kb[D:], a["L2_attn_x_proj_b"]],
        "L2x": [a[f"L2_xattn_W{n}"].T for n in "qkvo"] + [a[f"L2_xattn_b{n}"] for n in "qkvo"],
        "L3c": [a[f"L3_xattn_W{n}"] for n in "qkvo"] + [a[f"L3_xattn_b{n}"] for n in "qkvo"],
    }
    r = {}
    for n, (wq, wk, wv, wo, bq, bk, bv, bo) in att.items():
        t[f"{n}_wq"], t[f"{n}_wk"], t[f"{n}_wv"], t[f"{n}_wo"] = wq[:, perm], wk[:, perm], wv, wo
        if bq is not None:
            t[f"{n}_bq"], t[f"{n}_bk"], r[f"{n}_bv"] = bq[perm][:, None], bk[perm][:, None], bv
        r[f"{n}_bo"] = bo
    t["wf"] = a["L0_xattn_Wf"]
    t["g1"], t["b1"] = a["L0_xattn_g1"][:, None], a["L0_xattn_b1"][:, None]
    for n in ("g2", "b2", "g3", "b3"):
        t[n] = np.broadcast_to(a[f"L0_xattn_{n}"], (P, D))
    t["wscale"] = np.broadcast_to(a["L0_ffn_weight_scale"], (P, 1))
    for n in ("ln1", "lnx", "ln2"):
        t[f"{n}_g"], t[f"{n}_b"] = a[f"L2_attn_{n}_g"][:, None], a[f"L2_attn_{n}_b"][:, None]
    t["fc"] = a["L2_attn_fc_w"]
    t["fc_b"] = a["L2_attn_fc_b"].reshape(FT1, P).T
    t["mlp"] = a["L2_attn_mlp_proj_w"].reshape(FT1, P, D).transpose(1, 0, 2).reshape(P, FT1 * D)
    t["enc"] = a["L2_attn_encoder_hidden_states"][0].T
    t["wr1"], t["wr2"], t["wr3"] = a["L1_ffn_Wr"], a["L2_ffn_Wr"], a["L3_ffn_Wr"]
    t["e1_b1"] = a["L1_ffn_b1"].reshape(E1 * FT1, P).T
    t["e2_b1"] = a["L2_ffn_b1"].reshape(E2 * FT1, P).T
    t["e3_b1"] = np.concatenate([a["L3_ffn_Be1"], a["L3_ffn_bs1"][None]]).T
    t["l3_bq"] = a["L3_attn_in_proj_bias"][0:LP].reshape(LP // P, P).T
    t["l3_bk"] = a["L3_attn_in_proj_bias"][LP:2 * LP].reshape(LP // P, P).T
    r["bf"], r["q8_b"], r["mlp_b"] = a["L0_xattn_bf"], a["L0_ffn_bias"], a["L2_attn_mlp_proj_b"]
    r["br1"], r["br2"], r["br3"] = a["L1_ffn_br"], a["L2_ffn_br"], a["L3_ffn_br"]
    r["scorer"] = a["L2_attn_scorer_logits"][0]
    r["l3_bo"] = a["L3_attn_out_proj_bias"]

    def experts(w1, w2):
        n, _, hidden = w1.shape
        w2 = w2.reshape(n, hidden // P, P, D).transpose(0, 2, 1, 3).reshape(n, P, hidden)
        return np.concatenate([w1, w2], 2)

    e_b2 = np.zeros((32, 3, D), f)
    e_b2[0:E1, 0], e_b2[0:E2, 1] = a["L1_ffn_b2"], a["L2_ffn_b2"]
    e_b2[0:E3, 2] = np.concatenate([a["L3_ffn_Be2"], a["L3_ffn_bs2"][None]])
    mask = a["mask_1x1xSxS2_ik0"][0, 0]
    arrays = {
        "x": a["x"],
        "ctxT": a["ctx_1024"].transpose(2, 0, 1),
        "pack": np.concatenate([np.asarray(t[n], f).reshape(P, w) for n, w in PACKED], 1),
        "rows": np.concatenate([np.asarray(r[n], f).reshape(1, w) for n, w in ROWS], 1),
        "mask_q": mask.reshape(QT, P, SC).transpose(1, 0, 2).reshape(P, QT * SC),
        "mask_k": mask.T,
        "w_q8": a["L0_ffn_w_int8"].T,
        "e_b2": e_b2,
        "experts1": experts(a["L1_ffn_W1"], a["L1_ffn_W2"]),
        "experts2": experts(a["L2_ffn_W1"], a["L2_ffn_W2"]),
        "experts3": np.concatenate([experts(a["L3_ffn_We1"], a["L3_ffn_We2"]),
                                    experts(a["L3_ffn_ws1"][None], a["L3_ffn_ws2"][None])])
        .reshape(E3 // 4, 4, P, 2 * P).transpose(0, 2, 1, 3).reshape(E3 // 4, P, 8 * P),
        "in_w": a["L3_attn_in_proj_weight"].T,
        "out_w": a["L3_attn_out_proj_weight"].T.reshape(LP // P, P, D).transpose(1, 0, 2),
        "l3_bv": np.broadcast_to(a["L3_attn_in_proj_bias"][2 * LP:], (P, LP)),
    }
    arrays = {k: np.ascontiguousarray(v) for k, v in arrays.items()}
    nc = bacc.Bacc("TRN2", target_bir_lowering=False, num_devices=1)
    io = {k: nc.dram_tensor(f"{k}_dram", v.shape, mybir.dt.from_np(v.dtype), kind="ExternalInput").ap()
          for k, v in arrays.items()}
    io["out"] = nc.dram_tensor("out_dram", (B, S, D), F32, kind="ExternalOutput").ap()
    build(nc, io)
    got = run_bass_kernel_spmd(nc, [{f"{k}_dram": v for k, v in arrays.items()}], core_ids=[0])
    return got.results[0]["out_dram"]
```
